# Optimizing a Trainium2 kernel written in Bass

```python
import numpy as np
import jax
import jax.numpy as jnp

def _softmax(x, axis=-1):
    return jax.nn.softmax(x, axis=axis)

def _gelu(x):
    return jax.nn.gelu(x, approximate=True)

def _silu(x):
    return jax.nn.silu(x)

def _sigmoid(x):
    return jax.nn.sigmoid(x)

def _layernorm(x, axis=-1, eps=1e-05):
    m = jnp.mean(x, axis=axis, keepdims=True)
    v = jnp.var(x, axis=axis, keepdims=True)
    return (x - m) / jnp.sqrt(v + eps)

def _scatter_add(tgt, idx, src, axis=0):
    return tgt.at[idx].add(src)

def _segment_sum(src, seg, n):
    return jax.ops.segment_sum(src, seg, n)
kernel_name = 'mk_gnn_resnorm_d1_gnn_r8_cb563f'

def setup_inputs(seed: int=0):
    np.random.seed(seed)
    _w = jnp.asarray

    def _rec_inputs():
        import jax
        import jax.numpy as jnp
        _gk = jax.random.key(seed)
        x = -0.0008691 + 1 * jax.random.normal(jax.random.fold_in(_gk, 1), (12500, 128), jnp.float32)
        _s = jax.random.randint(jax.random.fold_in(_gk, 2), (100000,), 0, 12500, jnp.int32)
        _d = jax.random.randint(jax.random.fold_in(_gk, 3), (100000,), 0, 12500, jnp.int32)
        _loop = jnp.arange(12500, dtype=jnp.int32)
        src = jnp.concatenate([_s, _d, _loop])
        dst = jnp.concatenate([_d, _s, _loop])
        _o = jnp.argsort(dst, stable=True)
        src = src[_o]
        dst = dst[_o]
        return (x, src, dst)
    x, src, dst = _rec_inputs()

    def _L0_gnn_setup():
        import jax, jax.numpy as jnp
        import numpy as np
        N_NODES = 1250
        N_EDGES = 80000
        D_IN = 128
        D_OUT = 128
        key = jax.random.key(seed)
        ks = jax.random.split(key, 8)
        x = jax.random.normal(ks[0], (N_NODES, D_IN), dtype=jnp.float32)
        edge_index = jax.random.randint(ks[1], (2, N_EDGES), 0, N_NODES, dtype=jnp.int64)
        batch = jnp.zeros((N_NODES,), dtype=jnp.int64)
        s_in = 1.0 / np.sqrt(D_IN)
        s_out = 1.0 / np.sqrt(D_OUT)
        W_lin = jax.random.uniform(ks[2], (D_OUT, D_IN), jnp.float32, -s_in, s_in)
        b_lin = jax.random.uniform(ks[3], (D_OUT,), jnp.float32, -s_in, s_in)
        W_gate = jax.random.uniform(ks[4], (1, D_IN), jnp.float32, -s_in, s_in)
        b_gate = jax.random.uniform(ks[5], (1,), jnp.float32, -s_in, s_in)
        W_out = jax.random.uniform(ks[6], (D_OUT, D_OUT), jnp.float32, -s_out, s_out)
        b_out = jax.random.uniform(ks[7], (D_OUT,), jnp.float32, -s_out, s_out)
        return {'x': x, 'edge_index': edge_index, 'batch': batch, 'W_lin': W_lin, 'b_lin': b_lin, 'W_gate': W_gate, 'b_gate': b_gate, 'W_out': W_out, 'b_out': b_out}
    _L0_gnn_all = _L0_gnn_setup()
    _L0_gnn_in = {k: v for k, v in _L0_gnn_all.items() if k in ('W_lin', 'b_lin', 'W_gate', 'b_gate', 'W_out', 'b_out')}
    del _L0_gnn_all
    return {'x': x, 'src': src, 'dst': dst, 'L0_gnn_W_lin': _L0_gnn_in['W_lin'], 'L0_gnn_b_lin': _L0_gnn_in['b_lin'], 'L0_gnn_W_gate': _L0_gnn_in['W_gate'], 'L0_gnn_b_gate': _L0_gnn_in['b_gate'], 'L0_gnn_W_out': _L0_gnn_in['W_out'], 'L0_gnn_b_out': _L0_gnn_in['b_out']}

def reference(x, src, dst, L0_gnn_W_lin, L0_gnn_b_lin, L0_gnn_W_gate, L0_gnn_b_gate, L0_gnn_W_out, L0_gnn_b_out):
    import jax
    import jax.numpy as jnp

    def _L0_gnn_ref(x, edge_index, batch, W_lin, b_lin, W_gate, b_gate, W_out, b_out):
        import jax, jax.numpy as jnp
        import numpy as np
        N_NODES = 1250
        N_EDGES = 80000
        D_IN = 128
        D_OUT = 128
        row, col = (edge_index[0], edge_index[1])
        n = x.shape[0]
        messages = x[col]
        gate = messages @ W_gate.T + b_gate
        h = messages @ W_lin.T + b_lin
        g = gate[:, 0]
        seg_max = jax.ops.segment_max(g, row, num_segments=n)
        e = jnp.exp(g - seg_max[row])
        denom = jax.ops.segment_sum(e, row, num_segments=n) + 1e-16
        attn = (e / denom[row])[:, None]
        pooled = jax.ops.segment_sum(attn * h, row, num_segments=n)
        return pooled @ W_out.T + b_out
    edge_index = jnp.stack([src, dst])
    batch0 = jnp.zeros((12500,), jnp.int32)
    x = _layernorm(x + _L0_gnn_ref(x, edge_index, batch0, L0_gnn_W_lin, L0_gnn_b_lin, L0_gnn_W_gate, L0_gnn_b_gate, L0_gnn_W_out, L0_gnn_b_out), axis=-1)
    return x

_drawn_inputs = setup_inputs


def setup_inputs(seed=0):
    import zlib

    import numpy as np

    out = dict(_drawn_inputs(seed))
    spreads = {}
    factors = {}
    for name, (base, spread) in spreads.items():
        noise = np.random.default_rng([zlib.crc32(name.encode()), seed]).standard_normal(out[name].shape)
        drawn = base * np.exp(spread * noise) if base else spread * noise
        out[name] = jnp.asarray(drawn.astype(out[name].dtype))
    for name, factor in factors.items():
        out[name] = (out[name] * factor).astype(out[name].dtype)
    return out
```

```python
import numpy as np
import concourse.bass as bass
from concourse import mybir
from contextlib import ExitStack

F32 = mybir.dt.float32
BF16 = mybir.dt.bfloat16
I32 = mybir.dt.int32
ALU = mybir.AluOpType
ACT = mybir.ActivationFunctionType
AX = mybir.AxisListType

P = 128
NODES, FEAT, EDGES = 12500, 128, 212500
BLOCKS = -(-NODES // P)
LAST_ROWS = NODES - (BLOCKS - 1) * P

DST_BITS, PLACE_BITS = 14, 8
BLOCK_SHIFT = DST_BITS + PLACE_BITS
KEY_BASE = 0x40000000
PAD_PLACE = 255
DST_MASK, PLACE_MASK = (1 << DST_BITS) - 1, (1 << PLACE_BITS) - 1
LAST_KEY = KEY_BASE | (BLOCKS - 1) << BLOCK_SHIFT | PAD_PLACE << DST_BITS

LOG_COLS = 11
COLS = 1 << LOG_COLS
LOG_KEYS = LOG_COLS + 7
KEYS = P * COLS
EDGE_ROWS, EDGE_COLS = 125, 1700
TURN = COLS // P
BANK_SQUARES = 4

LO, HI, HCOLS = 16, 7, 4
HGROUPS = EDGE_COLS // HCOLS
HUNROLL = 17

T = 40
CHUNKS = 44
BATCH = 4
NB = T // BATCH
WIDTH = FEAT + 1
ROW = FEAT + 2
NODE_ROWS, NODE_COLS = 125, 100
GATE_COLS = 20
NEG = -1.0e30

GB = 7
GROUPS = BLOCKS // GB


def check_shapes():
    assert EDGE_ROWS * EDGE_COLS == EDGES and NODE_ROWS * NODE_COLS == NODES
    assert CHUNKS % 2 == 0 and CHUNKS * T >= (EDGES + BLOCKS * (P - 1)) // P and (CHUNKS + 1) * T * P < KEYS
    assert EDGE_COLS + BLOCKS <= COLS and LO * HI >= BLOCKS and BLOCKS % GB == 0 and GROUPS % 2 == 0


def as_float(bits):
    return float(np.array([bits], np.uint32).view(np.float32)[0])


def graph_attention(nc, x, src, dst, w_lin, b_lin, w_gate, b_gate, w_out, b_out, out):
    check_shapes()
    with ExitStack() as ctx:
        def sb(name, shape, dt=F32):
            return ctx.enter_context(nc.sbuf_tensor(name, shape, dt))

        def sem(name):
            return ctx.enter_context(nc.semaphore(name))

        table = nc.dram_tensor("node_table", (NODES, ROW), F32).ap()
        skeys = nc.dram_tensor("sorted_keys", (KEYS + 1,), I32).ap()

        rows_a, rows_b = sb("rows_a", [P, COLS]), sb("rows_b", [P, COLS])
        turn_a, turn_b = sb("turn_a", [P, COLS]), sb("turn_b", [P, COLS])
        src_i, dst_i = turn_a.ap().bitcast(I32), turn_b.ap().bitcast(I32)
        part_i = rows_b.ap().bitcast(I32)
        lohi_b = turn_b.ap().bitcast(BF16)
        nodes_sb = sb("nodes_sb", [P, 13000])
        node_rows = nodes_sb[0:NODE_ROWS, 0:NODE_COLS * ROW].rearrange("p (n f) -> p n f", f=ROW)
        sums = nodes_sb[:, 0:BLOCKS * WIDTH]
        arena = sb("arena", [P, 23 * EDGE_COLS // 2 + EDGE_COLS])
        onehot = arena[0:EDGE_ROWS, 0:23 * EDGE_COLS // 2].bitcast(BF16).rearrange("p (g c k) -> p g c k", c=LO + HI, k=HCOLS)
        part2_i = arena[0:EDGE_ROWS, 23 * EDGE_COLS // 2:23 * EDGE_COLS // 2 + EDGE_COLS].bitcast(I32)
        gathered_rows = [arena[:, k * T * ROW:(k + 1) * T * ROW].rearrange("p (t f) -> p t f", f=ROW) for k in range(2)]
        gate_prod = sb("gate_prod", [P, GATE_COLS, FEAT])
        gate_junk = sb("gate_junk", [P, FEAT])
        gate_sum = sb("gate_sum", [P, NODE_COLS])
        wg = sb("wg", [P, FEAT])
        bg = sb("bg", [P, 1])

        iota_i, iota_row = sb("iota_i", [P, P], I32), sb("iota_row", [P, P])
        part_idx_i, part_idx = sb("part_idx_i", [P, 1], I32), sb("part_idx", [P, 1])
        ident = sb("ident", [P, P])
        ones = sb("ones", [P, P])
        diag_i = sb("diag_i", [LO * HCOLS, HCOLS, LO], I32)
        diag_eq = sb("diag_eq", [LO * HCOLS, HCOLS, LO])
        same_col = sb("same_col", [LO * HCOLS, HCOLS])
        is_lo = sb("is_lo", [LO * HCOLS, LO])
        hist_kept = sb("hist_kept", [LO * HCOLS, HI, HCOLS])
        hist_sum = sb("hist_sum", [LO * HCOLS, HI])
        hist_spread = sb("hist_spread", [LO * HCOLS, HI, LO])
        padkey_i = sb("padkey_i", [P, BLOCKS], I32)
        padn_i = sb("padn_i", [P, BLOCKS], I32)
        padn_j = sb("padn_j", [P, BLOCKS], I32)
        pad_off = sb("pad_off", [P, BLOCKS])
        bit_i = sb("bit_i", [P, 9], I32)
        signs = sb("signs", [P, 9])
        flips = sb("flips", [P, 8])

        wl_sb, wo_sb, wo_t = sb("wl_sb", [P, P]), sb("wo_sb", [P, P]), sb("wo_t", [P, P])
        bl_col = sb("bl_col", [P, 1])
        wc_t = sb("wc_t", [P, P])
        bias2 = sb("bias2", [2, P])
        zero_key = sb("zero_key", [1, 1], I32)
        eps_col = sb("eps_col", [P, 1])

        k3 = [sb(f"k3_{k}", [T, 3, P], I32) for k in range(2)]
        node_i, node_f = sb("node_i", [T, 3, P], I32), sb("node_f", [T, 3, P])
        dst_r, place_r = sb("dst_r", [T, P], I32), sb("place_r", [T, P], I32)
        prev_place_i, block_i = sb("prev_place_i", [T, 1], I32), sb("block_i", [T, 1], I32)
        dst_f, place_f = sb("dst_f", [T, P]), sb("place_f", [T, P])
        prev_place = [sb(f"prev_place{k}", [T, 1]) for k in range(2)]
        sums_at = sb("sums_at", [T, 1])
        differs = sb("differs", [T, 2, P])
        pen = [sb(f"pen{k}", [T, 2, P]) for k in range(2)]
        pen_tile = [sb(f"pen_tile{k}", [T, P]) for k in range(2)]
        goes_on = [sb(f"goes_on{k}", [T, 1]) for k in range(2)]
        gather_at = [sb(f"gather_at{k}", [P, T], I32) for k in range(2)]
        place_t = [sb(f"place_t{k}", [P, T]) for k in range(2)]
        offs = [sb(f"offs{k}", [1, T], I32) for k in range(2)]
        tile_pen = [sb(f"tile_pen{k}", [1, T]) for k in range(2)]
        run_max, run_max2, seg_max = sb("run_max", [T, P]), sb("run_max2", [T, P]), sb("seg_max", [T, P])
        carry = sb("carry", [1, T + 1])
        carry_col = sb("carry_col", [T, 1])
        drop = sb("drop", [T, 1])
        expo = sb("expo", [T, 2, P])
        weights = [sb(f"weights{k}", [P, 2, T]) for k in range(2)]
        spread = sb("spread", [P, 2 * BATCH, P])

        den = sb("den", [P, GB])
        def again(buf, k, width):
            return buf[:, k * (COLS // 2):k * (COLS // 2) + GB * width].rearrange("p (c f) -> p c f", f=width)

        x_grp, y_grp, pooled = ([again(buf, k, width) for k in range(2)]
                                for buf, width in ((rows_a, FEAT), (rows_b, FEAT), (turn_a, ROW)))
        pooled_t, resid = again(turn_b, 0, FEAT), again(turn_b, 1, FEAT)
        share_t = arena[0:2, 0:GB * P].rearrange("p (c f) -> p c f", f=P)
        stats = sb("stats", [P, GB, 6])
        mean_var = sb("mean_var", [P, GB, 2])
        std, inv_std = sb("std", [P, GB]), sb("inv_std", [P, GB])

        bank = [ctx.enter_context(nc.psum_tensor(f"bank{k}", [P, 512], F32)) for k in range(8)]
        hist_ps = bank[7][0:LO * HCOLS, 0:HI * HCOLS].rearrange("p (h k) -> p h k", k=HCOLS)
        count_ps = bank[6][:, 0:HI * LO]
        gate_rows = bank[4][0:T, 0:P]
        tile_block_ps, tile_pen_ps, tile_max_ps = bank[6][0:1, 256:256 + T], bank[6][0:1, 384:384 + T], bank[5][0:1, 128:128 + T]
        carry_ps = bank[5][0:T, 192:193]
        prep_ps = bank[6][:, 0:2 * T].rearrange("p (a t) -> p a t", a=2)
        expo_ps = bank[7][:, 0:2 * T].rearrange("p (a t) -> p a t", a=2)

        def tile_ps(slot):
            return bank[slot // 2][:, (slot % 2) * 256:(slot % 2) * 256 + WIDTH]

        src_loaded, dst_loaded, x_loaded, weights_loaded = sem("src_loaded"), sem("dst_loaded"), sem("x_loaded"), sem("weights_loaded")
        iotas_ready, consts_ready = sem("iotas_ready"), sem("consts_ready")
        prod_ready, prod_used, gates_ready, ones_ready = sem("prod_ready"), sem("prod_used"), sem("gates_ready"), sem("ones_ready")
        table_stored, keys_stored, zero_ready = sem("table_stored"), sem("keys_stored"), sem("zero_ready")
        onehots_ready, hist_ready, spread_ready, counts_ready = sem("onehots_ready"), sem("hist_ready"), sem("spread_ready"), sem("counts_ready")
        wo_turned, wo_copied, wc_ready, wc_copied = sem("wo_turned"), sem("wo_copied"), sem("wc_ready"), sem("wc_copied")
        to_turn, turned, turn_copied = sem("to_turn"), sem("turned"), sem("turn_copied")
        keys_sorted = sem("keys_sorted")
        k3_loaded = [sem(f"k3_loaded{k}") for k in range(2)]
        k3_used = sem("k3_used")
        prep_done, prep_turned, prep_copied = sem("prep_done"), sem("prep_turned"), sem("prep_copied")
        rows_gathered = [sem(f"rows_gathered{k}") for k in range(2)]
        gather_buf_free = sem("gather_buf_free")
        gates_turned, run_max_done, tile_max_turned, carry_done, carry_turned = (
            sem("gates_turned"), sem("run_max_done"), sem("tile_max_turned"), sem("carry_done"), sem("carry_turned"))
        expo_done, expo_turned, weights_ready = sem("expo_done"), sem("expo_turned"), sem("weights_ready")
        spread_done, tiles_summed, psum_free = sem("spread_done"), sem("tiles_summed"), sem("psum_free")
        x_in = [sem(f"x_in{k}") for k in range(2)]
        pooled_ready, pooled_turned, pooled_copied, y_ready, y_used = (
            sem("pooled_ready"), sem("pooled_turned"), sem("pooled_copied"), sem("y_ready"), sem("y_used"))
        var_ready, std_ready, out_ready = sem("var_ready"), sem("std_ready"), sem("out_ready")
        stored = [sem(f"stored{k}") for k in range(2)]

        block = ctx.enter_context(nc.Block())

        def group_of(a, g, parts):
            if parts == "whole":
                return a[bass.ds(g * GB * P, GB * P), :].rearrange("(c p) f -> p c f", p=P)
            if parts == "full":
                return a[g * GB * P:g * GB * P + (GB - 1) * P, :].rearrange("(c p) f -> p c f", p=P)
            return a[NODES - LAST_ROWS:NODES, :]

        @block.sync
        def _(sp):
            sp.dma_start(src_i[0:EDGE_ROWS, 0:EDGE_COLS], src.rearrange("(p n) -> p n", n=EDGE_COLS)).then_inc(src_loaded, 16)
            sp.dma_start(dst_i[0:EDGE_ROWS, 0:EDGE_COLS], dst.rearrange("(p n) -> p n", n=EDGE_COLS)).then_inc(dst_loaded, 16)
            sp.wait_ge(gates_ready, 1)
            sp.wait_ge(ones_ready, 1)
            sp.dma_start(table.rearrange("(p n) f -> p n f", n=NODE_COLS), node_rows).then_inc(table_stored, 16)
            sp.wait_ge(zero_ready, 1)
            sp.dma_start(skeys[0:1].rearrange("(a n) -> a n", a=1), zero_key[:, :]).then_inc(keys_stored, 16)
            sp.wait_ge(keys_sorted, 1)
            sp.dma_start(skeys[1:1 + KEYS].rearrange("(p n) -> p n", n=COLS), rows_a.ap().bitcast(I32)).then_inc(keys_stored, 16)
            sp.wait_ge(keys_stored, 32)

            def load_chunk(i, par):
                for shift in range(3):
                    sp.dma_start(k3[par][:, shift, :],
                                 skeys[bass.ds(i * (T * P) + shift, T * P)].rearrange("(t n) -> t n", n=P)).then_inc(k3_loaded[par], 16)

            load_chunk(0, 0)
            with sp.Fori(0, CHUNKS // 2) as j:
                sp.wait_ge(k3_used, 2 * j + 1)
                load_chunk(2 * j + 1, 1)
                sp.wait_ge(k3_used, 2 * j + 2)
                load_chunk(2 * j + 2, 0)

            def load_x(g, par, last=False):
                if last:
                    sp.dma_start(x_grp[par][:, 0:GB - 1, :], group_of(x, g, "full")).then_inc(x_in[par], 16)
                    sp.dma_start(x_grp[par][0:LAST_ROWS, GB - 1, :], group_of(x, g, "rest")).then_inc(x_in[par], 16)
                else:
                    sp.dma_start(x_grp[par][:, :, :], group_of(x, g, "whole")).then_inc(x_in[par], 16)

            def store(g, par, last=False):
                sp.wait_ge(out_ready, g + 1)
                if last:
                    sp.dma_start(group_of(out, g, "full"), y_grp[par][:, 0:GB - 1, :]).then_inc(stored[par], 16)
                    sp.dma_start(group_of(out, g, "rest"), y_grp[par][0:LAST_ROWS, GB - 1, :]).then_inc(stored[par], 16)
                else:
                    sp.dma_start(group_of(out, g, "whole"), y_grp[par][:, :, :]).then_inc(stored[par], 16)

            load_x(0, 0)
            load_x(1, 1)
            with sp.Fori(0, GROUPS // 2 - 2) as j:
                for par in range(2):
                    store(2 * j + par, par)
                    load_x(2 * j + (par + 2), par)
            store(GROUPS - 4, 0)
            load_x(GROUPS - 2, 0)
            store(GROUPS - 3, 1)
            load_x(GROUPS - 1, 1, last=True)
            store(GROUPS - 2, 0)
            store(GROUPS - 1, 1, last=True)
            sp.wait_ge(stored[0], 16 * (GROUPS // 2))
            sp.wait_ge(stored[1], 16 * (GROUPS // 2 + 1))
            sp.wait_ge(table_stored, 16)

        @block.gpsimd
        def _(pool):
            pool.iota(iota_i[:, :], [[1, P]], base=0, channel_multiplier=0)
            pool.iota(part_idx_i[:, :], [[1, 1]], base=0, channel_multiplier=1)
            pool.iota(padkey_i[:, :], [[1, BLOCKS]], base=0, channel_multiplier=0)
            pool.iota(diag_i[:, :, :], [[-1, HCOLS], [-HCOLS, LO]], base=0, channel_multiplier=1)
            pool.drain().then_inc(iotas_ready, 1)
            pool.wait_ge(x_loaded, 16)
            pool.wait_ge(weights_loaded, 16 * 6)
            pool.memset(node_rows[:, :, FEAT:FEAT + 1], 1.0).then_inc(ones_ready, 1)
            for c in range(NODE_COLS // GATE_COLS):
                if c > 0:
                    pool.wait_ge(prod_used, c)
                pool.tensor_tensor(gate_prod[0:NODE_ROWS], node_rows[:, c * GATE_COLS:(c + 1) * GATE_COLS, 0:FEAT],
                                   wg[0:NODE_ROWS].unsqueeze(1).to_broadcast([NODE_ROWS, GATE_COLS, FEAT]),
                                   ALU.mult).then_inc(prod_ready, 1)
            pool.wait_ge(table_stored, 16)
            with pool.Fori(0, CHUNKS // 2) as j:
                for par in range(2):
                    pool.wait_ge(prep_copied, 2 * j + (par + 1))
                    pool.wait_ge(gather_buf_free, 2 * j + (par + 1))
                    pool.nop(nofuse=True)
                    for t in range(T):
                        pool.indirect_dma_start(out=gathered_rows[par][:, t, :], out_offset=None, in_=table[:, :],
                                                in_offset=bass.IndirectOffsetOnAxis(ap=gather_at[par][:, t:t + 1], axis=0)
                                                ).then_inc(rows_gathered[par], 16)

        @block.scalar
        def _(act):
            act.dma_start(node_rows[:, :, 0:FEAT], x.rearrange("(p n) f -> p n f", n=NODE_COLS)).then_inc(x_loaded, 16)
            act.dma_start(wg[:, :], w_gate.partition_broadcast(P)).then_inc(weights_loaded, 16)
            act.dma_start(bg[:, :], b_gate.rearrange("(a n) -> a n", a=1).partition_broadcast(P)).then_inc(weights_loaded, 16)
            act.dma_start(wl_sb[:, :], w_lin).then_inc(weights_loaded, 16)
            act.dma_start(wo_sb[:, :], w_out).then_inc(weights_loaded, 16)
            act.dma_start(bl_col[:, :], b_lin.rearrange("(n a) -> n a", a=1)).then_inc(weights_loaded, 16)
            act.dma_start(bias2[1:2, :], b_out.rearrange("(a n) -> a n", a=1)).then_inc(weights_loaded, 16)
            act.wait_ge(wo_turned, 1)
            act.activation(wo_t[:, :], bank[4][:, 0:P], ACT.Copy).then_inc(wo_copied, 1)
            act.wait_ge(wc_ready, 1)
            act.activation(wc_t[:, :], bank[5][:, 0:P], ACT.Copy)
            act.activation(bias2[0:1, :], bank[5][0:1, P:2 * P], ACT.Copy).then_inc(wc_copied, 1)
            act.wait_ge(weights_loaded, 16 * 6)
            for c in range(NODE_COLS // GATE_COLS):
                act.wait_ge(prod_ready, c + 1)
                for n in range(GATE_COLS):
                    at = c * GATE_COLS + n
                    last = act.activation(gate_junk[0:NODE_ROWS], gate_prod[0:NODE_ROWS, n, :], ACT.Copy,
                                          accum_out=gate_sum[0:NODE_ROWS, at:at + 1])
                    act.drain()
                act.drain().then_inc(prod_used, 1)
            act.activation(node_rows[:, :, FEAT + 1], gate_sum[0:NODE_ROWS, :], ACT.Identity,
                           bias=bg[0:NODE_ROWS, 0:1]).then_inc(gates_ready, 1)
            for r in range(2 * (LOG_KEYS - LOG_COLS)):
                into = turn_a if r % 2 == 0 else rows_a
                for b in range(BANK_SQUARES):
                    act.wait_ge(turned, BANK_SQUARES * r + b + 1)
                    act.activation(into[:, b * 512:(b + 1) * 512], bank[b][:, :], ACT.Copy).then_inc(turn_copied, 1)

            def copy_prep(i, par):
                act.wait_ge(prep_turned, i + 1)
                act.activation(gather_at[par][:, :], prep_ps[:, 0, :], ACT.Copy)
                act.activation(place_t[par][:, :], prep_ps[:, 1, :], ACT.Copy)
                act.activation(offs[par][:, :], tile_block_ps, ACT.Copy)
                act.activation(tile_pen[par][:, :], tile_pen_ps, ACT.Copy)
                act.drain().then_inc(prep_copied, 1)

            def weigh(i, par):
                act.wait_ge(expo_turned, i + 1)
                act.activation(weights[par][:, :, :], expo_ps, ACT.Exp).then_inc(weights_ready, 1)

            copy_prep(0, 0)
            with act.Fori(0, CHUNKS // 2) as j:
                for par in range(2):
                    copy_prep(2 * j + (par + 1), 1 - par)
                    weigh(2 * j + par, par)

            def finish(g, par):
                act.wait_ge(pooled_turned, g + 1)
                act.activation(pooled_t[:, 0:4, :], bank[0][:, :].rearrange("p (c f) -> p c f", f=P), ACT.Copy)
                act.activation(pooled_t[:, 4:GB, :], bank[1][:, 0:(GB - 4) * P].rearrange("p (c f) -> p c f", f=P), ACT.Copy)
                act.activation(share_t[:, 0:4, :], bank[2][0:2, :].rearrange("p (c f) -> p c f", f=P), ACT.Copy)
                act.activation(share_t[:, 4:GB, :], bank[3][0:2, 0:(GB - 4) * P].rearrange("p (c f) -> p c f", f=P), ACT.Copy)
                act.drain().then_inc(pooled_copied, 1)
                act.wait_ge(var_ready, g + 1)
                act.activation(std[:, :], mean_var[:, :, 1], ACT.Sqrt, bias=eps_col[:, 0:1]).then_inc(std_ready, 1)

            with act.Fori(0, GROUPS // 2) as j:
                for par in range(2):
                    finish(2 * j + par, par)

        @block.tensor
        def _(pe):
            pe.wait_ge(weights_loaded, 16 * 6)
            pe.wait_ge(consts_ready, 1)
            pe.nop(nofuse=True)
            pe.transpose(bank[4][:, 0:P], wo_sb[:, :], ident[:, :]).then_inc(wo_turned, 1)
            pe.wait_ge(wo_copied, 1)
            pe.matmul(bank[5][:, 0:P], lhsT=wl_sb[:, :], rhs=wo_t[:, :], start=True, stop=True)
            pe.matmul(bank[5][0:1, P:2 * P], lhsT=bl_col[:, :], rhs=wo_t[:, :], start=True, stop=True).then_inc(wc_ready, 1)
            pe.wait_ge(onehots_ready, 1)

            def count(at, start=False, stop=False):
                return pe.matmul(hist_ps, lhsT=onehot[:, bass.ds(at, 1), 0:LO, :].rearrange("p g c k -> p (g c k)"),
                                 rhs=onehot[:, bass.ds(at, 1), LO:LO + HI, :].rearrange("p g c k -> p (g c k)"),
                                 start=start, stop=stop)

            count(0, start=True)
            for u in range(1, HUNROLL):
                count(u)
            with pe.Fori(1, HGROUPS // HUNROLL - 1) as j:
                for u in range(HUNROLL):
                    count(j * HUNROLL + u)
            for u in range(HUNROLL):
                last = count(HGROUPS - HUNROLL + u, stop=u == HUNROLL - 1)
            last.then_inc(hist_ready, 1)
            pe.wait_ge(spread_ready, 1)
            pe.matmul(count_ps, lhsT=ones[0:LO * HCOLS, :], rhs=hist_spread[:, :, :].rearrange("p h l -> p (h l)"),
                      start=True, stop=True).then_inc(counts_ready, 1)
            for r in range(2 * (LOG_KEYS - LOG_COLS)):
                k = LOG_COLS + 1 + r // 2
                from_ = rows_b if r % 2 == 0 else (turn_a if (k - LOG_COLS) % 2 == 0 else turn_b)
                pe.wait_ge(to_turn, r + 1)
                for q in range(TURN):
                    last = pe.transpose(bank[q // BANK_SQUARES][:, (q % BANK_SQUARES) * P:(q % BANK_SQUARES + 1) * P],
                                        from_[:, q * P:(q + 1) * P], ident[:, :])
                    if q % BANK_SQUARES == BANK_SQUARES - 1:
                        last.then_inc(turned, 1)
            pe.drain().then_inc(gather_buf_free, 2)

            def turn_prep(i):
                pe.wait_ge(prep_done, i + 1)
                if not (isinstance(i, int) and i == 0):
                    pe.wait_ge(prep_copied, i)
                pe.nop(nofuse=True)
                pe.transpose(prep_ps[:, 0, :], dst_f[:, :], ident[0:T, 0:T])
                pe.transpose(prep_ps[:, 1, :], place_f[:, :], ident[0:T, 0:T])
                pe.transpose(tile_block_ps, sums_at[:, :], ident[0:T, 0:T])

            def turn_pen(i, par):
                pe.transpose(tile_pen_ps, pen_tile[par][:, P - 1:P], ident[0:T, 0:T]).then_inc(prep_turned, 1)

            turn_prep(0)
            turn_pen(0, 0)
            with pe.Fori(0, CHUNKS // 2) as j:
                for par in range(2):
                    i = 2 * j + par
                    turn_prep(i + 1)
                    turn_pen(i + 1, 1 - par)
                    pe.wait_ge(rows_gathered[par], 16 * T * j + 16 * T)
                    pe.nop(nofuse=True)
                    pe.transpose(gate_rows, gathered_rows[par][:, :, FEAT + 1], ident[:, :]).then_inc(gates_turned, 1)
                    pe.wait_ge(run_max_done, i + 1)
                    pe.nop(nofuse=True)
                    pe.transpose(tile_max_ps, run_max[:, P - 1:P], ident[0:T, 0:T]).then_inc(tile_max_turned, 1)
                    pe.wait_ge(carry_done, i + 1)
                    pe.nop(nofuse=True)
                    pe.transpose(carry_ps, carry[0:1, 0:T], ident[0:1, 0:1]).then_inc(carry_turned, 1)
                    pe.wait_ge(expo_done, i + 1)
                    pe.nop(nofuse=True)
                    pe.transpose(expo_ps[:, 0, :], expo[:, 0, :], ident[0:T, 0:T])
                    pe.transpose(expo_ps[:, 1, :], expo[:, 1, :], ident[0:T, 0:T]).then_inc(expo_turned, 1)
                    for b in range(NB):
                        pe.wait_ge(spread_done, i * NB + (b + 1))
                        pe.wait_ge(psum_free, i * NB + (b + 1))
                        for u in range(BATCH):
                            slot = (b % 2) * BATCH + u
                            last = pe.matmul(tile_ps(slot), lhsT=spread[:, slot, :],
                                             rhs=gathered_rows[par][:, b * BATCH + u, 0:WIDTH], start=True, stop=True)
                        last.then_inc(tiles_summed, 1)
                    pe.drain().then_inc(gather_buf_free, 1)

            def finish(g, par):
                pe.wait_ge(pooled_ready, g + 1)
                pe.nop(nofuse=True)
                for c in range(GB):
                    pe.transpose(bank[c // 4][:, (c % 4) * P:(c % 4 + 1) * P], pooled[par][:, c, 0:FEAT], ident[:, :])
                    last = pe.transpose(bank[2 + c // 4][0:2, (c % 4) * P:(c % 4 + 1) * P], pooled[par][:, c, FEAT:ROW], ident[:, :])
                last.then_inc(pooled_turned, 1)
                pe.wait_ge(pooled_copied, g + 1)
                pe.wait_ge(y_used, g + 1)
                for c in range(GB):
                    to = bank[4 + c // 4][:, (c % 4) * P:(c % 4 + 1) * P]
                    pe.matmul(to, lhsT=pooled_t[:, c, :], rhs=wc_t[:, :], start=True, stop=False)
                    last = pe.matmul(to, lhsT=share_t[:, c, :], rhs=bias2[:, :], start=False, stop=True)
                last.then_inc(y_ready, 1)

            pe.wait_ge(wc_copied, 1)
            with pe.Fori(0, GROUPS // 2) as j:
                for par in range(2):
                    finish(2 * j + par, par)

        @block.vector
        def _(dve):
            dve.memset(zero_key[:, :], 0).then_inc(zero_ready, 1)
            dve.memset(rows_a[:, :], as_float(LAST_KEY))
            dve.memset(ones[:, :], 1.0)
            dve.memset(eps_col[:, :], 1e-5)
            dve.memset(carry[:, :], NEG)
            dve.wait_ge(iotas_ready, 1)
            dve.tensor_copy(iota_row[:, :], iota_i[:, :])
            dve.tensor_copy(part_idx[:, :], part_idx_i[:, :])
            dve.tensor_scalar(diag_eq[:, :, :], diag_i[:, :, :], 0.0, None, ALU.is_equal)
            dve.tensor_scalar(padkey_i[:, :], padkey_i[:, :], BLOCK_SHIFT, KEY_BASE | PAD_PLACE << DST_BITS,
                              ALU.logical_shift_left, ALU.bitwise_or)
            dve.memset(bit_i[:, :], 0)
            dve.drain()
            dve.tensor_scalar(ident[:, :], iota_row[:, :], part_idx[:, 0:1], None, ALU.is_equal)
            dve.tensor_reduce(same_col[:, :], diag_eq[:, :, :], AX.X, ALU.add)
            dve.tensor_reduce(is_lo[:, :], diag_eq[:, :, :].rearrange("p k l -> p l k"), AX.X, ALU.add)
            for k in range(LOG_KEYS - LOG_COLS):
                dve.tensor_scalar(bit_i[:, k + 1:k + 2], part_idx_i[:, :], k, 1, ALU.logical_shift_right, ALU.bitwise_and)
            dve.drain()
            dve.tensor_scalar(signs[:, :], bit_i[:, :], -2.0, 1.0, ALU.mult, ALU.add)
            dve.drain().then_inc(consts_ready, 1)
            dve.memset(signs[:, 8:9], 1.0)
            dve.drain()
            dve.tensor_tensor(flips[:, :], signs[:, 1:9], signs[:, 0:8], ALU.mult)

            e = slice(0, EDGE_ROWS), slice(0, EDGE_COLS)
            dve.wait_ge(src_loaded, 16)
            dve.tensor_scalar(part_i[e], src_i[e], P - 1, DST_BITS, ALU.bitwise_and, ALU.logical_shift_left)
            dve.tensor_scalar(part2_i, src_i[e], 7, BLOCK_SHIFT, ALU.logical_shift_right, ALU.logical_shift_left)
            dve.drain()
            dve.scalar_tensor_tensor(part_i[e], part_i[e], KEY_BASE, part2_i, ALU.bitwise_or, ALU.bitwise_or)
            dve.drain()
            dve.wait_ge(dst_loaded, 16)
            keys_i = rows_a.ap().bitcast(I32)
            dve.tensor_tensor(keys_i[e], part_i[e], dst_i[e], ALU.bitwise_or)
            dve.drain()
            dve.tensor_scalar(part_i[e], src_i[e], 7, LO - 1, ALU.logical_shift_right, ALU.bitwise_and)
            dve.tensor_scalar(part2_i, src_i[e], 11, None, ALU.logical_shift_right)
            dve.drain()
            lo_b, hi_b = (lohi_b[0:EDGE_ROWS, k * EDGE_COLS:(k + 1) * EDGE_COLS].rearrange("p (g k) -> p g k", k=HCOLS) for k in range(2))
            dve.tensor_copy(lo_b, part_i[e].rearrange("p (g k) -> p g k", k=HCOLS))
            dve.tensor_copy(hi_b, part2_i.rearrange("p (g k) -> p g k", k=HCOLS))
            dve.drain()
            for c in range(LO):
                dve.tensor_scalar(onehot[:, :, c, :], lo_b, float(c), None, ALU.is_equal)
            for c in range(HI):
                dve.tensor_scalar(onehot[:, :, LO + c, :], hi_b, float(c), None, ALU.is_equal)
            dve.drain().then_inc(onehots_ready, 1)
            dve.wait_ge(hist_ready, 1)
            q = LO * HCOLS
            dve.tensor_tensor(hist_kept[:, :, :], hist_ps, same_col[:, :].unsqueeze(1).to_broadcast([q, HI, HCOLS]), ALU.mult)
            dve.drain()
            dve.tensor_reduce(hist_sum[:, :], hist_kept[:, :, :], AX.X, ALU.add)
            dve.drain()
            dve.tensor_tensor(hist_spread[:, :, :], hist_sum[:, :].unsqueeze(2).to_broadcast([q, HI, LO]),
                              is_lo[:, :].unsqueeze(1).to_broadcast([q, HI, LO]), ALU.mult).then_inc(spread_ready, 1)
            dve.wait_ge(counts_ready, 1)
            dve.tensor_scalar(padn_i[:, :], count_ps[:, 0:BLOCKS], -1.0, None, ALU.mult)
            dve.drain()
            dve.tensor_scalar(padn_j[:, :], padn_i[:, :], P - 1, None, ALU.bitwise_and)
            dve.drain()
            dve.tensor_scalar(pad_off[:, :], padn_j[:, :], part_idx[:, 0:1], as_float(LAST_KEY), ALU.is_le, ALU.mult)
            dve.drain()
            dve.tensor_tensor(rows_a[:, EDGE_COLS:EDGE_COLS + BLOCKS], padkey_i.ap().bitcast(F32), pad_off[:, :], ALU.max)
            dve.drain()

            def exchange(a, b, s, k=None):
                if k is not None:
                    form = dict(d=2, b=1 << (k - s - 1), t=2, j=1 << s)
                    va, vb = (v[:, :].rearrange("p (a d b t j) -> p a d b t j", **form) for v in (a, b))
                    for d in range(2):
                        lo, hi = va[:, :, d, :, 0, :], va[:, :, d, :, 1, :]
                        dve.tensor_tensor(vb[:, :, d, :, 0, :], lo, hi, ALU.max if d else ALU.min)
                        dve.tensor_tensor(vb[:, :, d, :, 1, :], lo, hi, ALU.min if d else ALU.max)
                else:
                    va, vb = (v[:, :].rearrange("p (a t j) -> p a t j", t=2, j=1 << s) for v in (a, b))
                    dve.tensor_tensor(vb[:, :, 0, :], va[:, :, 0, :], va[:, :, 1, :], ALU.min)
                    dve.tensor_tensor(vb[:, :, 1, :], va[:, :, 0, :], va[:, :, 1, :], ALU.max)
                dve.drain()

            bufs = [rows_a, rows_b]
            at = 0
            for k in range(1, LOG_COLS):
                for s in reversed(range(k)):
                    exchange(bufs[at], bufs[1 - at], s, k)
                    at = 1 - at
            r = 0
            for k in range(LOG_COLS, LOG_KEYS + 1):
                dve.tensor_scalar(bufs[1 - at][:, :], bufs[at][:, :], flips[:, k - LOG_COLS:k - LOG_COLS + 1], None, ALU.mult)
                at = 1 - at
                if k > LOG_COLS:
                    assert at == 1
                    dve.drain().then_inc(to_turn, 1)
                    dve.wait_ge(turn_copied, BANK_SQUARES * (r + 1))
                    turns = [turn_a, turn_b]
                    tat = 0
                    for s in reversed(range(k - LOG_COLS)):
                        exchange(turns[tat], turns[1 - tat], s)
                        tat = 1 - tat
                    dve.drain().then_inc(to_turn, 1)
                    dve.wait_ge(turn_copied, BANK_SQUARES * (r + 2))
                    r += 2
                    at = 0
                else:
                    dve.drain()
                for s in reversed(range(LOG_COLS)):
                    exchange(bufs[at], bufs[1 - at], s)
                    at = 1 - at
                if at == 1 and k == LOG_KEYS or at == 1 and k < LOG_KEYS:
                    dve.tensor_copy(rows_a[:, :], rows_b[:, :])
                    dve.drain()
                    at = 0
            dve.drain().then_inc(keys_sorted, 1)
            dve.wait_ge(table_stored, 16)
            dve.memset(sums, 0.0)
            for k in range(2):
                dve.memset(pooled[k][:, :, ROW - 1:ROW], 1.0)
            dve.drain().then_inc(psum_free, 2)

            def prepare(i, j_uses, par):
                dve.wait_ge(k3_loaded[par], j_uses * 48 + 48)
                own = k3[par][:, 1, :]
                dve.tensor_scalar(node_i[:, :, :], k3[par][:, :, :], DST_BITS, None, ALU.logical_shift_right)
                dve.tensor_scalar(dst_r[:, :], own, DST_MASK, None, ALU.bitwise_and)
                dve.tensor_scalar(place_r[:, :], own, DST_BITS, PLACE_MASK, ALU.logical_shift_right, ALU.bitwise_and)
                dve.tensor_scalar(prev_place_i[:, :], k3[par][:, 0, 0:1], DST_BITS, PLACE_MASK, ALU.logical_shift_right, ALU.bitwise_and)
                dve.tensor_scalar(block_i[:, :], k3[par][:, 1, 0:1], BLOCK_SHIFT, 127, ALU.logical_shift_right, ALU.bitwise_and)
                dve.drain().then_inc(k3_used, 1)
                if not (isinstance(i, int) and i == 0):
                    dve.wait_ge(prep_turned, i)
                dve.tensor_copy(node_f[:, :, :], node_i[:, :, :])
                dve.tensor_copy(dst_f[:, :], dst_r[:, :])
                dve.tensor_copy(place_f[:, :], place_r[:, :])
                dve.tensor_copy(prev_place[par][:, :], prev_place_i[:, :])
                dve.tensor_scalar(sums_at[:, :], block_i[:, :], float(WIDTH), None, ALU.mult)
                dve.drain()
                dve.tensor_scalar(pen_tile[par][:, :], node_f[:, 1, :], node_f[:, 0, 0:1], NEG, ALU.not_equal, ALU.mult)
                dve.tensor_tensor(differs[:, :, :], node_f[:, 1:2, :].to_broadcast([T, 2, P]), node_f[:, 0:3:2, :], ALU.not_equal)
                dve.drain()
                dve.tensor_scalar(pen[par][:, :, :], differs[:, :, :], NEG, None, ALU.mult)
                dve.tensor_scalar(goes_on[par][:, :], pen_tile[par][:, 0:1], 0.0, None, ALU.is_equal)
                dve.drain().then_inc(prep_done, 1)

            def softmax(i, par):
                dve.wait_ge(gates_turned, i + 1)
                dve.tensor_tensor_scan(run_max[:, :], pen[par][:, 0, :], gate_rows, NEG, ALU.add, ALU.max)
                dve.drain().then_inc(run_max_done, 1)
                dve.wait_ge(tile_max_turned, i + 1)
                dve.tensor_tensor_scan(carry[0:1, 1:T + 1], tile_pen[par][:, :], tile_max_ps, carry[0:1, 0:1], ALU.add, ALU.max)
                dve.drain().then_inc(carry_done, 1)
                dve.wait_ge(carry_turned, i + 1)
                dve.tensor_copy(carry_col[:, :], carry_ps)
                dve.tensor_copy(carry[0:1, 0:1], carry[0:1, T:T + 1])
                dve.drain()
                dve.scalar_tensor_tensor(run_max2[:, :], pen_tile[par][:, :], carry_col[:, 0:1], run_max[:, :], ALU.add, ALU.max)
                dve.drain()
                dve.tensor_tensor_scan(seg_max[:, ::-1], pen[par][:, 1, ::-1], run_max2[:, ::-1], NEG, ALU.add, ALU.max)
                dve.drain()
                dve.tensor_tensor(expo[:, 0, :], gate_rows, seg_max[:, :], ALU.subtract)
                dve.scalar_tensor_tensor(drop[:, :], carry_col[:, :], seg_max[:, 0:1], goes_on[par][:, :], ALU.subtract, ALU.mult)
                dve.drain()
                dve.tensor_scalar(expo[:, 1, :], iota_row[0:T, :], prev_place[par][:, 0:1], drop[:, 0:1], ALU.is_equal, ALU.mult)
                dve.drain().then_inc(expo_done, 1)

            def add_batch(i, par, b, at_cols):
                dve.wait_ge(tiles_summed, i * NB + (b + 1))
                for u in range(BATCH):
                    t = b * BATCH + u
                    here = sums[:, bass.ds(at_cols[t], WIDTH)]
                    dve.scalar_tensor_tensor(here, here, weights[par][:, 1, t:t + 1], tile_ps((b % 2) * BATCH + u), ALU.mult, ALU.add)
                    if u < BATCH - 1:
                        dve.drain()
                dve.drain().then_inc(psum_free, 1)

            prepare(0, 0, 0)
            with dve.Fori(0, CHUNKS // 2) as j:
                for par in range(2):
                    i = 2 * j + par
                    prepare(i + 1, j + par, 1 - par)
                    softmax(i, par)
                    dve.wait_ge(weights_ready, i + 1)
                    dve.wait_ge(prep_copied, i + 1)
                    dve.nop(nofuse=True)
                    at_cols = {}
                    for b in range(NB):
                        if b % 2 == 0:
                            n = 2 * BATCH if b + 1 < NB else BATCH
                            got = nc.values_load_multi_w_load_instructions(
                                offs[par][0:1, b * BATCH:b * BATCH + n], engines=[mybir.EngineType.DVE], min_val=0,
                                max_val=(BLOCKS - 1) * WIDTH, skip_runtime_bounds_check_because="a block times the width")[1]
                            new_cols = {b * BATCH + m: got[m] for m in range(n)}
                        for u in range(BATCH):
                            t = b * BATCH + u
                            ins = dve.tensor_scalar(spread[:, (b % 2) * BATCH + u, :], iota_row[:, :], place_t[par][:, t:t + 1],
                                                    weights[par][:, 0, t:t + 1], ALU.is_equal, ALU.mult)
                        ins.then_inc(spread_done, 1)
                        if b > 0:
                            add_batch(i, par, b - 1, at_cols)
                        at_cols.update(new_cols)
                    add_batch(i, par, NB - 1, at_cols)

            def finish(g, par, x_count):
                here = sums[:, bass.ds(g * GB * WIDTH, GB * WIDTH)].rearrange("p (c w) -> p c w", w=WIDTH)
                dve.tensor_scalar(den[:, :], here[:, :, FEAT], 1e-16, None, ALU.add)
                dve.drain()
                dve.reciprocal(den[:, :], den[:, :])
                dve.drain()
                dve.tensor_tensor(pooled[par][:, :, 0:WIDTH], here, den[:, :].unsqueeze(2).to_broadcast([P, GB, WIDTH]),
                                  ALU.mult).then_inc(pooled_ready, 1)
                dve.wait_ge(x_in[par], x_count)
                dve.wait_ge(y_ready, g + 1)
                for lo, hi, bk in ((0, 4, 4), (4, GB, 5)):
                    ps = bank[bk][:, 0:(hi - lo) * P].rearrange("p (c f) -> p c f", f=P)
                    dve.tensor_tensor(resid[:, lo:hi, :], ps, x_grp[par][:, lo:hi, :], ALU.add)
                dve.drain().then_inc(y_used, 1)
                for c in range(GB):
                    dve.bn_stats(stats[:, c, :], resid[:, c, :])
                dve.drain()
                for c in range(GB):
                    dve.bn_aggr(mean_var[:, c, :], stats[:, c, :])
                dve.drain().then_inc(var_ready, 1)
                dve.wait_ge(std_ready, g + 1)
                dve.reciprocal(inv_std[:, :], std[:, :])
                dve.drain()
                for c in range(GB):
                    dve.tensor_scalar(y_grp[par][:, c, :], resid[:, c, :], mean_var[:, c, 0:1], inv_std[:, c:c + 1],
                                      ALU.subtract, ALU.mult)
                dve.drain().then_inc(out_ready, 1)

            dve.memset(den[:, :], 0.0).then_inc(y_used, 1)
            dve.drain()
            with dve.Fori(0, GROUPS // 2 - 1) as j:
                for par in range(2):
                    finish(2 * j + par, par, 16 * j + 16)
            finish(GROUPS - 2, 0, 16 * (GROUPS // 2))
            finish(GROUPS - 1, 1, 16 * (GROUPS // 2 + 1))


_INS = ['x', 'src', 'dst', 'L0_gnn_W_lin', 'L0_gnn_b_lin', 'L0_gnn_W_gate', 'L0_gnn_b_gate', 'L0_gnn_W_out', 'L0_gnn_b_out']


def kernel(**inputs):
    import concourse.bacc as bacc
    from concourse.bass_utils import run_bass_kernel_spmd as run
    nc = bacc.Bacc("TRN2", target_bir_lowering=False, num_devices=1)
    arrays, args = {}, []
    for name in _INS:
        a = np.ascontiguousarray(inputs[name])
        arrays[f"in_{name}"] = a
        args.append(nc.dram_tensor(f"in_{name}", a.shape, mybir.dt.from_np(a.dtype), kind="ExternalInput").ap())
    out = nc.dram_tensor("out_0", (NODES, FEAT), F32, kind="ExternalOutput").ap()
    graph_attention(nc, *args, out)
    r = run(nc, [arrays], core_ids=[0])
    return r.results[0]["out_0"]
```

```python
import numpy as np
import concourse.bass as bass
from concourse import mybir
from contextlib import ExitStack

F32 = mybir.dt.float32
BF16 = mybir.dt.bfloat16
I32 = mybir.dt.int32
ALU = mybir.AluOpType
ACT = mybir.ActivationFunctionType
AX = mybir.AxisListType
ENGINE = mybir.EngineType

P = 128
NODES, FEAT, EDGES = 12500, 128, 212500
BLOCKS = -(-NODES // P)
LAST_ROWS = NODES - (BLOCKS - 1) * P

DST_BITS, PLACE_BITS = 14, 8
BLOCK_SHIFT = DST_BITS + PLACE_BITS
KEY_BASE = 0x40000000
PAD_PLACE = 255
DST_MASK, PLACE_MASK = (1 << DST_BITS) - 1, (1 << PLACE_BITS) - 1
LAST_KEY = KEY_BASE | (BLOCKS - 1) << BLOCK_SHIFT | PAD_PLACE << DST_BITS

LOG_COLS, LOG_ROWS = 8, 7
BIG = 7
LOG_BIG = LOG_COLS + LOG_ROWS
LOG_KEYS = LOG_BIG + 3
BCOLS = 1 << LOG_COLS
COLS = BIG * BCOLS
KEYS = P * COLS
HALF = COLS // 2
BANK = 512
PARTS = [(0, 4), (4, 7)]
LAG = 2

MAIN_COLS = 1656
REST_ROWS, REST_COLS = 14, 38
PAD_AT = MAIN_COLS + REST_COLS
TAIL_ROWS = 16

LO, HI, HCOLS = 16, 7, 4
EDGE_COLS = 1696
HGROUPS = EDGE_COLS // HCOLS

T = 40
CHUNKS = 44
BATCH = 4
NB = T // BATCH
WIDTH = FEAT + 1
ROW = FEAT + 2
NODE_ROWS, NODE_COLS = 125, 100
GATE_COLS = 10
NEG = -1.0e30

GB = 7
GROUPS = BLOCKS // GB


def check_shapes():
    assert P * MAIN_COLS + REST_ROWS * REST_COLS == EDGES and NODE_ROWS * NODE_COLS == NODES
    assert CHUNKS % 4 == 0 and CHUNKS * T >= (EDGES + BLOCKS * (P - 1)) // P and (CHUNKS + 1) * T * P < KEYS + TAIL_ROWS * P
    assert PAD_AT + BLOCKS <= COLS and PAD_AT <= EDGE_COLS <= COLS and PARTS[1][0] * BCOLS <= MAIN_COLS and HALF >= GB * FEAT
    assert LO * HI >= BLOCKS and BLOCKS % GB == 0 and GROUPS % 2 == 0


def as_float(bits):
    return float(np.array([bits], np.uint32).view(np.float32)[0])


def graph_attention(nc, x, src, dst, w_lin, b_lin, w_gate, b_gate, w_out, b_out, out):
    check_shapes()
    with ExitStack() as ctx:
        def sb(name, shape, dt=F32):
            return ctx.enter_context(nc.sbuf_tensor(name, shape, dt))

        def sem(name):
            return ctx.enter_context(nc.semaphore(name))

        table = nc.dram_tensor("node_table", (NODES, ROW), F32).ap()
        skeys = nc.dram_tensor("sorted_keys", (1 + KEYS + TAIL_ROWS * P,), I32).ap()

        rows_a, rows_b = sb("rows_a", [P, COLS]), sb("rows_b", [P, COLS])
        turn_a, turn_b = sb("turn_a", [P, COLS]), sb("turn_b", [P, COLS])
        src_i, dst_i = turn_a.ap().bitcast(I32), turn_b.ap().bitcast(I32)
        part_i = rows_b.ap().bitcast(I32)
        lohi_b = turn_b.ap().bitcast(BF16)
        nodes_sb = sb("nodes_sb", [P, 13000])
        node_rows = nodes_sb[0:NODE_ROWS, 0:NODE_COLS * ROW].rearrange("p (n f) -> p n f", f=ROW)
        sums = nodes_sb[:, 0:BLOCKS * WIDTH]
        arena = sb("arena", [P, 23 * EDGE_COLS // 2 + EDGE_COLS])
        onehot = arena[:, 0:23 * EDGE_COLS // 2].bitcast(BF16).rearrange("p (g c k) -> p g c k", c=LO + HI, k=HCOLS)
        part2_i = arena[:, 23 * EDGE_COLS // 2:23 * EDGE_COLS // 2 + EDGE_COLS].bitcast(I32)
        gathered_rows = [arena[:, k * T * ROW:(k + 1) * T * ROW].rearrange("p (t f) -> p t f", f=ROW) for k in range(2)]
        gate_prod = sb("gate_prod", [P, GATE_COLS, FEAT])
        gate_junk = sb("gate_junk", [P, FEAT])
        gate_sum = sb("gate_sum", [P, NODE_COLS])
        wg = sb("wg", [P, FEAT])
        bg = sb("bg", [P, 1])

        iota_i, iota_row = sb("iota_i", [P, P], I32), sb("iota_row", [P, P])
        part_idx_i, part_idx = sb("part_idx_i", [P, 1], I32), sb("part_idx", [P, 1])
        ident = sb("ident", [P, P])
        ones = sb("ones", [P, P])
        diag_i = sb("diag_i", [LO * HCOLS, HCOLS, LO], I32)
        diag_eq = sb("diag_eq", [LO * HCOLS, HCOLS, LO])
        same_col = sb("same_col", [LO * HCOLS, HCOLS])
        is_lo = sb("is_lo", [LO * HCOLS, LO])
        hist_kept = sb("hist_kept", [LO * HCOLS, HI, HCOLS])
        hist_sum = sb("hist_sum", [LO * HCOLS, HI])
        hist_spread = sb("hist_spread", [LO * HCOLS, HI, LO])
        padkey_i = sb("padkey_i", [P, BLOCKS], I32)
        padn_i = sb("padn_i", [P, BLOCKS], I32)
        padn_j = sb("padn_j", [P, BLOCKS], I32)
        pad_off = sb("pad_off", [P, BLOCKS])
        bit_i = sb("bit_i", [P, LOG_ROWS + 1], I32)
        signs = sb("signs", [P, LOG_ROWS + 1])
        flips = sb("flips", [P, LOG_ROWS])

        wl_sb, wo_sb, wo_t = sb("wl_sb", [P, P]), sb("wo_sb", [P, P]), sb("wo_t", [P, P])
        bl_col = sb("bl_col", [P, 1])
        wc_t = sb("wc_t", [P, P])
        bias2 = sb("bias2", [2, P])
        zero_key = sb("zero_key", [1, 1], I32)
        eps_col = sb("eps_col", [P, 1])

        k3 = [sb(f"k3_{k}", [T, 3, P], I32) for k in range(2)]
        node_i, node_f = sb("node_i", [T, 3, P], I32), sb("node_f", [T, 3, P])
        dst_r, place_r = sb("dst_r", [T, P], I32), sb("place_r", [T, P], I32)
        prev_place_i, block_i = sb("prev_place_i", [T, 1], I32), sb("block_i", [T, 1], I32)
        dst_f, place_f = sb("dst_f", [T, P]), sb("place_f", [T, P])
        prev_place = [sb(f"prev_place{k}", [T, 1]) for k in range(2)]
        sums_at = sb("sums_at", [T, 1])
        differs = sb("differs", [T, 2, P])
        pen = [sb(f"pen{k}", [T, 2, P]) for k in range(2)]
        pen_tile = [sb(f"pen_tile{k}", [T, P]) for k in range(2)]
        goes_on = [sb(f"goes_on{k}", [T, 1]) for k in range(2)]
        gather_at = [sb(f"gather_at{k}", [P, T], I32) for k in range(2)]
        place_t = [sb(f"place_t{k}", [P, T]) for k in range(2)]
        offs = [sb(f"offs{k}", [1, T], I32) for k in range(2)]
        tile_pen = [sb(f"tile_pen{k}", [1, T]) for k in range(2)]
        run_max, run_max2, seg_max = sb("run_max", [T, P]), sb("run_max2", [T, P]), sb("seg_max", [T, P])
        carry = sb("carry", [1, T + 1])
        carry_col = sb("carry_col", [T, 1])
        drop = sb("drop", [T, 1])
        expo = sb("expo", [T, 2, P])
        weights = [sb(f"weights{k}", [P, 2, T]) for k in range(2)]
        spread = sb("spread", [P, 2 * BATCH, P])

        den = sb("den", [P, GB])
        def again(buf, k, width):
            return buf[:, k * HALF:k * HALF + GB * width].rearrange("p (c f) -> p c f", f=width)

        x_grp, y_grp, pooled = ([again(buf, k, width) for k in range(2)]
                                for buf, width in ((rows_a, FEAT), (rows_b, FEAT), (turn_a, FEAT)))
        resid = [again(turn_b, k, FEAT) for k in range(2)]
        pooled_t = [arena[:, k * HALF:k * HALF + GB * P].rearrange("p (c f) -> p c f", f=P) for k in range(2)]
        share = [sb(f"share{k}", [P, GB, 2]) for k in range(2)]
        share_t = [arena[0:2 * GB, (2 + k) * HALF:(2 + k) * HALF + P] for k in range(2)]
        bias_at_i, bias_at = sb("bias_at_i", [2, GB, 2 * GB], I32), sb("bias_at", [2, GB, 2 * GB])
        bias_of = sb("bias_of", [2 * GB, GB, P])
        stats = sb("stats", [P, GB, 6])
        mean_var = [sb(f"mean_var{k}", [P, GB, 2]) for k in range(2)]
        std, inv_std, shift = ([sb(f"{name}{k}", [P, GB]) for k in range(2)] for name in ("std", "inv_std", "shift"))

        bank = [ctx.enter_context(nc.psum_tensor(f"bank{k}", [P, 512], F32)) for k in range(8)]
        hist_ps = bank[7][0:LO * HCOLS, 0:HI * HCOLS].rearrange("p (h k) -> p h k", k=HCOLS)
        count_ps = bank[6][:, 0:HI * LO]
        gate_rows = bank[4][0:T, 0:P]
        tile_block_ps, tile_pen_ps, tile_max_ps = bank[6][0:1, 256:256 + T], bank[6][0:1, 384:384 + T], bank[5][0:1, 128:128 + T]
        carry_ps = bank[5][0:T, 192:193]
        prep_ps = bank[6][:, 0:2 * T].rearrange("p (a t) -> p a t", a=2)
        expo_ps = bank[7][:, 0:2 * T].rearrange("p (a t) -> p a t", a=2)

        def tile_ps(slot):
            return bank[slot // 2][:, (slot % 2) * 256:(slot % 2) * 256 + WIDTH]

        src_loaded, dst_loaded, x_loaded, weights_loaded = sem("src_loaded"), sem("dst_loaded"), sem("x_loaded"), sem("weights_loaded")
        iotas_ready, consts_ready = sem("iotas_ready"), sem("consts_ready")
        prod_ready, prod_used, gates_ready, ones_ready = sem("prod_ready"), sem("prod_used"), sem("gates_ready"), sem("ones_ready")
        table_stored, keys_stored, zero_ready = sem("table_stored"), sem("keys_stored"), sem("zero_ready")
        onehots_ready, hist_ready, spread_ready, counts_ready = sem("onehots_ready"), sem("hist_ready"), sem("spread_ready"), sem("counts_ready")
        wo_turned, wo_copied, wc_ready, wc_copied = sem("wo_turned"), sem("wo_copied"), sem("wc_ready"), sem("wc_copied")
        bias_spread, bias_copied = sem("bias_spread"), sem("bias_copied")
        steps_done, turned, turn_copied = ([sem(f"{name}{g}") for g in range(2)] for name in ("steps_done", "turned", "turn_copied"))
        blank_ready = sem("blank_ready")
        k3_loaded = [sem(f"k3_loaded{k}") for k in range(2)]
        k3_used = sem("k3_used")
        prep_done, prep_turned, prep_copied = sem("prep_done"), sem("prep_turned"), sem("prep_copied")
        rows_gathered = [sem(f"rows_gathered{k}") for k in range(2)]
        gather_buf_free = sem("gather_buf_free")
        gates_turned, run_max_done, tile_max_turned, carry_done, carry_turned = (
            sem("gates_turned"), sem("run_max_done"), sem("tile_max_turned"), sem("carry_done"), sem("carry_turned"))
        expo_done, expo_turned, weights_ready = sem("expo_done"), sem("expo_turned"), sem("weights_ready")
        spread_done, tiles_summed, sums_added = sem("spread_done"), sem("tiles_summed"), sem("sums_added")
        x_in = [sem(f"x_in{k}") for k in range(2)]
        pooled_ready, pooled_turned, pooled_copied, y_ready, y_used = (
            sem("pooled_ready"), sem("pooled_turned"), sem("pooled_copied"), sem("y_ready"), sem("y_used"))
        var_ready, std_ready, norm_ready, out_ready = sem("var_ready"), sem("std_ready"), sem("norm_ready"), sem("out_ready")
        stored = [sem(f"stored{k}") for k in range(2)]

        to_cols, to_rows = {}, {}
        steps = LOG_COLS * (LOG_COLS - 1) // 2
        for k in range(LOG_COLS, LOG_KEYS + 1):
            steps += 1 + max(0, k - LOG_BIG)
            to_cols[k] = steps
            steps += min(k - LOG_COLS, LOG_ROWS)
            to_rows[k] = steps
            steps += LOG_COLS
        all_steps = steps
        turning = range(LOG_COLS + 1, LOG_KEYS + 1)

        def cols_of(g):
            return slice(PARTS[g][0] * BCOLS, PARTS[g][1] * BCOLS)

        def banks_of(k, back, g):
            lo, hi = PARTS[g][0] * BCOLS, PARTS[g][1] * BCOLS
            for n in range(2):
                at = lo + n * BANK
                yield bank[4 * back + 2 * g + n], at, min(BANK, hi - at), 4 * (k - LOG_COLS - 1) + 2 * back + n + 1

        def loop(engine, start, end):
            return nc.Fori(start, end, engines=[engine], hint_back_edge=True)

        block = ctx.enter_context(nc.Block())

        def group_of(a, g, parts):
            if parts == "whole":
                return a[bass.ds(g * GB * P, GB * P), :].rearrange("(c p) f -> p c f", p=P)
            if parts == "full":
                return a[g * GB * P:g * GB * P + (GB - 1) * P, :].rearrange("(c p) f -> p c f", p=P)
            return a[NODES - LAST_ROWS:NODES, :]

        @block.sync
        def _(sp):
            main, rest = slice(0, P * MAIN_COLS), slice(P * MAIN_COLS, EDGES)
            sp.dma_start(src_i[:, 0:MAIN_COLS], src[main].rearrange("(p n) -> p n", n=MAIN_COLS)).then_inc(src_loaded, 16)
            sp.wait_ge(blank_ready, 1)
            sp.dma_start(src_i[0:REST_ROWS, MAIN_COLS:PAD_AT], src[rest].rearrange("(p n) -> p n", n=REST_COLS)).then_inc(src_loaded, 16)
            sp.dma_start(dst_i[:, 0:MAIN_COLS], dst[main].rearrange("(p n) -> p n", n=MAIN_COLS)).then_inc(dst_loaded, 16)
            sp.dma_start(dst_i[0:REST_ROWS, MAIN_COLS:PAD_AT], dst[rest].rearrange("(p n) -> p n", n=REST_COLS)).then_inc(dst_loaded, 16)
            sp.dma_start(node_rows[:, :, 0:FEAT], x.rearrange("(p n) f -> p n f", n=NODE_COLS)).then_inc(x_loaded, 16)
            sp.wait_ge(gates_ready, 1)
            sp.wait_ge(ones_ready, 1)
            sp.dma_start(table.rearrange("(p n) f -> p n f", n=NODE_COLS), node_rows).then_inc(table_stored, 16)
            sp.wait_ge(zero_ready, 1)
            sp.dma_start(skeys[0:1].rearrange("(a n) -> a n", a=1), zero_key[:, :]).then_inc(keys_stored, 16)
            sp.dma_start(skeys[1 + KEYS:].rearrange("(p n) -> p n", n=P), iota_i[0:TAIL_ROWS, :]).then_inc(keys_stored, 16)
            for g in range(2):
                sp.wait_ge(steps_done[g], all_steps)
                lo, hi = PARTS[g]
                sp.dma_start(skeys[1 + lo * P * BCOLS:1 + hi * P * BCOLS].rearrange("(b p c) -> p b c", p=P, c=BCOLS),
                             rows_a.ap().bitcast(I32)[:, cols_of(g)].rearrange("p (b c) -> p b c", c=BCOLS)).then_inc(keys_stored, 16)
            sp.wait_ge(keys_stored, 64)

            def load_chunk(i, par):
                for shift in range(3):
                    sp.dma_start(k3[par][:, shift, :],
                                 skeys[bass.ds(i * (T * P) + shift, T * P)].rearrange("(t n) -> t n", n=P)).then_inc(k3_loaded[par], 16)

            load_chunk(0, 0)
            with sp.Fori(0, CHUNKS // 2) as j:
                sp.wait_ge(k3_used, 2 * j + 1)
                load_chunk(2 * j + 1, 1)
                sp.wait_ge(k3_used, 2 * j + 2)
                load_chunk(2 * j + 2, 0)

            def load_x(g, par, last=False):
                if last:
                    sp.dma_start(x_grp[par][:, 0:GB - 1, :], group_of(x, g, "full")).then_inc(x_in[par], 16)
                    sp.dma_start(x_grp[par][0:LAST_ROWS, GB - 1, :], group_of(x, g, "rest")).then_inc(x_in[par], 16)
                else:
                    sp.dma_start(x_grp[par][:, :, :], group_of(x, g, "whole")).then_inc(x_in[par], 16)

            def store(g, par, last=False):
                sp.wait_ge(out_ready, g + 1)
                if last:
                    sp.dma_start(group_of(out, g, "full"), y_grp[par][:, 0:GB - 1, :]).then_inc(stored[par], 16)
                    sp.dma_start(group_of(out, g, "rest"), y_grp[par][0:LAST_ROWS, GB - 1, :]).then_inc(stored[par], 16)
                else:
                    sp.dma_start(group_of(out, g, "whole"), y_grp[par][:, :, :]).then_inc(stored[par], 16)

            load_x(0, 0)
            load_x(1, 1)
            with sp.Fori(0, GROUPS // 2 - 2) as j:
                for par in range(2):
                    store(2 * j + par, par)
                    load_x(2 * j + (par + 2), par)
            store(GROUPS - 4, 0)
            load_x(GROUPS - 2, 0)
            store(GROUPS - 3, 1)
            load_x(GROUPS - 1, 1, last=True)
            store(GROUPS - 2, 0)
            store(GROUPS - 1, 1, last=True)
            sp.wait_ge(stored[0], 16 * (GROUPS // 2))
            sp.wait_ge(stored[1], 16 * (GROUPS // 2 + 1))
            sp.wait_ge(table_stored, 16)

        @block.gpsimd
        def _(pool):
            pool.iota(iota_i[:, :], [[1, P]], base=0, channel_multiplier=0)
            pool.iota(part_idx_i[:, :], [[1, 1]], base=0, channel_multiplier=1)
            pool.iota(padkey_i[:, :], [[1, BLOCKS]], base=0, channel_multiplier=0)
            pool.iota(diag_i[:, :, :], [[-1, HCOLS], [-HCOLS, LO]], base=0, channel_multiplier=1)
            pool.iota(bias_at_i[:, :, :], [[-2, GB], [1, 2 * GB]], base=0, channel_multiplier=-1)
            pool.drain().then_inc(iotas_ready, 1)
            pool.wait_ge(x_loaded, 16)
            pool.wait_ge(weights_loaded, 16 * 6)
            pool.memset(node_rows[:, :, FEAT:FEAT + 1], 1.0).then_inc(ones_ready, 1)
            for c in range(NODE_COLS // GATE_COLS):
                if c > 0:
                    pool.wait_ge(prod_used, c)
                pool.tensor_tensor(gate_prod[0:NODE_ROWS], node_rows[:, c * GATE_COLS:(c + 1) * GATE_COLS, 0:FEAT],
                                   wg[0:NODE_ROWS].unsqueeze(1).to_broadcast([NODE_ROWS, GATE_COLS, FEAT]),
                                   ALU.mult).then_inc(prod_ready, 1)
            pool.wait_ge(table_stored, 16)
            with loop(ENGINE.Pool, 0, CHUNKS // 4) as j:
                for c in range(4):
                    par = c % 2
                    pool.wait_ge(prep_copied, 4 * j + (c + 1))
                    pool.wait_ge(gather_buf_free, 4 * j + (c + 1))
                    pool.nop(nofuse=True)
                    for t in range(T):
                        pool.indirect_dma_start(out=gathered_rows[par][:, t, :], out_offset=None, in_=table[:, :],
                                                in_offset=bass.IndirectOffsetOnAxis(ap=gather_at[par][:, t:t + 1], axis=0)
                                                ).then_inc(rows_gathered[par], 16)

        @block.scalar
        def _(act):
            act.dma_start(wg[:, :], w_gate.partition_broadcast(P)).then_inc(weights_loaded, 16)
            act.dma_start(bg[:, :], b_gate.rearrange("(a n) -> a n", a=1).partition_broadcast(P)).then_inc(weights_loaded, 16)
            act.dma_start(wl_sb[:, :], w_lin).then_inc(weights_loaded, 16)
            act.dma_start(wo_sb[:, :], w_out).then_inc(weights_loaded, 16)
            act.dma_start(bl_col[:, :], b_lin.rearrange("(n a) -> n a", a=1)).then_inc(weights_loaded, 16)
            act.dma_start(bias2[1:2, :], b_out.rearrange("(a n) -> a n", a=1)).then_inc(weights_loaded, 16)
            act.wait_ge(wo_turned, 1)
            act.activation(wo_t[:, :], bank[4][:, 0:P], ACT.Copy).then_inc(wo_copied, 1)
            act.wait_ge(wc_ready, 1)
            act.activation(wc_t[:, :], bank[5][:, 0:P], ACT.Copy)
            act.activation(bias2[0:1, :], bank[5][0:1, P:2 * P], ACT.Copy).then_inc(wc_copied, 1)
            act.wait_ge(bias_spread, 1)
            for c, n in ((0, 4), (4, GB - 4)):
                last = act.activation(bias_of[:, c:c + n, :], bank[c // 4][0:2 * GB, 0:n * P].rearrange("p (c f) -> p c f", f=P), ACT.Copy)
            last.then_inc(bias_copied, 1)
            act.wait_ge(weights_loaded, 16 * 6)
            for c in range(NODE_COLS // GATE_COLS):
                act.wait_ge(prod_ready, c + 1)
                for n in range(GATE_COLS):
                    at = c * GATE_COLS + n
                    last = act.activation(gate_junk[0:NODE_ROWS], gate_prod[0:NODE_ROWS, n, :], ACT.Copy,
                                          accum_out=gate_sum[0:NODE_ROWS, at:at + 1])
                    act.drain()
                act.drain().then_inc(prod_used, 1)
            act.activation(node_rows[:, :, FEAT + 1], gate_sum[0:NODE_ROWS, :], ACT.Identity,
                           bias=bg[0:NODE_ROWS, 0:1]).then_inc(gates_ready, 1)
            for k in turning:
                for back, into in ((0, turn_a), (1, rows_a)):
                    for g in range(2):
                        for ps, at, n, filled in banks_of(k, back, g):
                            act.wait_ge(turned[g], filled)
                            act.activation(into[:, at:at + n], ps[:, 0:n], ACT.Copy).then_inc(turn_copied[g], 1)

            def copy_prep(i, par):
                act.wait_ge(prep_turned, i + 1)
                act.activation(gather_at[par][:, :], prep_ps[:, 0, :], ACT.Copy)
                act.activation(place_t[par][:, :], prep_ps[:, 1, :], ACT.Copy)
                act.activation(offs[par][:, :], tile_block_ps, ACT.Copy)
                act.activation(tile_pen[par][:, :], tile_pen_ps, ACT.Copy)
                act.drain().then_inc(prep_copied, 1)

            def weigh(i, par):
                act.wait_ge(expo_turned, i + 1)
                act.activation(weights[par][:, :, :], expo_ps, ACT.Exp).then_inc(weights_ready, 1)

            copy_prep(0, 0)
            with loop(ENGINE.Activation, 0, CHUNKS // 2) as j:
                for par in range(2):
                    copy_prep(2 * j + (par + 1), 1 - par)
                    weigh(2 * j + par, par)

            def copy_pooled(g, par):
                act.wait_ge(pooled_turned, g + 1)
                for c, n in ((0, 4), (4, GB - 4)):
                    act.activation(pooled_t[par][:, c:c + n, :], bank[c // 4][:, 0:n * P].rearrange("p (c f) -> p c f", f=P), ACT.Copy)
                act.activation(share_t[par], bank[2][0:2 * GB, 0:P], ACT.Copy)
                act.drain().then_inc(pooled_copied, 1)

            def take_root(g, par):
                act.wait_ge(var_ready, g + 1)
                act.activation(std[par][:, :], mean_var[par][:, :, 1], ACT.Sqrt, bias=eps_col[:, 0:1]).then_inc(std_ready, 1)

            def normalise(g, par, stores):
                act.wait_ge(norm_ready, g + 1)
                if stores is not None:
                    act.wait_ge(stored[par], stores)
                for c in range(GB):
                    act.activation(y_grp[par][:, c, :], resid[par][:, c, :], ACT.Identity,
                                   scale=inv_std[par][:, c:c + 1], bias=shift[par][:, c:c + 1])
                act.drain().then_inc(out_ready, 1)

            copy_pooled(0, 0)
            copy_pooled(1, 1)

            def step(g, par, stores, more=True):
                if more:
                    copy_pooled(g + 2, par)
                take_root(g, par)
                normalise(g, par, stores)

            step(0, 0, None)
            step(1, 1, None)
            with act.Fori(1, GROUPS // 2 - 1) as j:
                step(2 * j, 0, 16 * j)
                step(2 * j + 1, 1, 16 * j)
            step(GROUPS - 2, 0, 16 * (GROUPS // 2 - 1), more=False)
            step(GROUPS - 1, 1, 16 * (GROUPS // 2 - 1), more=False)

        @block.tensor
        def _(pe):
            pe.wait_ge(weights_loaded, 16 * 6)
            pe.wait_ge(consts_ready, 1)
            pe.nop(nofuse=True)
            pe.transpose(bank[4][:, 0:P], wo_sb[:, :], ident[:, :]).then_inc(wo_turned, 1)
            pe.wait_ge(wo_copied, 1)
            pe.matmul(bank[5][:, 0:P], lhsT=wl_sb[:, :], rhs=wo_t[:, :], start=True, stop=True)
            pe.matmul(bank[5][0:1, P:2 * P], lhsT=bl_col[:, :], rhs=wo_t[:, :], start=True, stop=True).then_inc(wc_ready, 1)
            pe.wait_ge(wc_copied, 1)
            for c in range(GB):
                last = pe.matmul(bank[c // 4][0:2 * GB, (c % 4) * P:(c % 4 + 1) * P], lhsT=bias_at[:, c, :], rhs=bias2[:, :],
                                 start=True, stop=True)
            last.then_inc(bias_spread, 1)
            pe.wait_ge(onehots_ready, 1)

            for g in range(HGROUPS):
                last = pe.matmul(hist_ps, lhsT=onehot[:, g, 0:LO, :].rearrange("p c k -> p (c k)"),
                                 rhs=onehot[:, g, LO:LO + HI, :].rearrange("p c k -> p (c k)"),
                                 start=g == 0, stop=g == HGROUPS - 1)
            last.then_inc(hist_ready, 1)
            pe.wait_ge(spread_ready, 1)
            pe.matmul(count_ps, lhsT=ones[0:LO * HCOLS, :], rhs=hist_spread[:, :, :].rearrange("p h l -> p (h l)"),
                      start=True, stop=True).then_inc(counts_ready, 1)
            pe.wait_ge(bias_copied, 1)
            for k in turning:
                for back in range(2):
                    if back:
                        from_ = (turn_a, turn_b)[min(k - LOG_COLS, LOG_ROWS) % 2]
                    else:
                        from_ = (rows_a, rows_b)[max(0, k - LOG_BIG) % 2]
                    for g in range(2):
                        pe.wait_ge(steps_done[g], (to_rows if back else to_cols)[k])
                        for ps, at, n, _ in banks_of(k, back, g):
                            for q in range(0, n, P):
                                last = pe.transpose(ps[:, q:q + P], from_[:, at + q:at + q + P], ident[:, :])
                            last.then_inc(turned[g], 1)
            pe.drain().then_inc(gather_buf_free, 2)

            def turn_prep(i):
                pe.wait_ge(prep_done, i + 1)
                if not (isinstance(i, int) and i == 0):
                    pe.wait_ge(prep_copied, i)
                pe.nop(nofuse=True)
                pe.transpose(prep_ps[:, 0, :], dst_f[:, :], ident[0:T, 0:T])
                pe.transpose(prep_ps[:, 1, :], place_f[:, :], ident[0:T, 0:T])
                pe.transpose(tile_block_ps, sums_at[:, :], ident[0:T, 0:T])

            def turn_pen(i, par):
                pe.transpose(tile_pen_ps, pen_tile[par][:, P - 1:P], ident[0:T, 0:T]).then_inc(prep_turned, 1)

            turn_prep(0)
            turn_pen(0, 0)
            with loop(ENGINE.PE, 0, CHUNKS // 2) as j:
                for par in range(2):
                    i = 2 * j + par
                    turn_prep(i + 1)
                    turn_pen(i + 1, 1 - par)
                    pe.wait_ge(rows_gathered[par], 16 * T * j + 16 * T)
                    pe.nop(nofuse=True)
                    pe.transpose(gate_rows, gathered_rows[par][:, :, FEAT + 1], ident[:, :]).then_inc(gates_turned, 1)
                    pe.wait_ge(run_max_done, i + 1)
                    pe.nop(nofuse=True)
                    pe.transpose(tile_max_ps, run_max[:, P - 1:P], ident[0:T, 0:T]).then_inc(tile_max_turned, 1)
                    pe.wait_ge(carry_done, i + 1)
                    pe.nop(nofuse=True)
                    pe.transpose(carry_ps, carry[0:1, 0:T], ident[0:1, 0:1]).then_inc(carry_turned, 1)
                    pe.wait_ge(expo_done, i + 1)
                    pe.nop(nofuse=True)
                    pe.transpose(expo_ps[:, 0, :], expo[:, 0, :], ident[0:T, 0:T])
                    pe.transpose(expo_ps[:, 1, :], expo[:, 1, :], ident[0:T, 0:T]).then_inc(expo_turned, 1)
                    for b in range(NB):
                        pe.wait_ge(spread_done, i * NB + (b + 1))
                        pe.wait_ge(sums_added, i * T + (b + 1) * BATCH)
                        for u in range(BATCH):
                            slot = (b % 2) * BATCH + u
                            last = pe.matmul(tile_ps(slot), lhsT=spread[:, slot, :],
                                             rhs=gathered_rows[par][:, b * BATCH + u, 0:WIDTH], start=True, stop=True)
                        last.then_inc(tiles_summed, 1)
                    pe.drain().then_inc(gather_buf_free, 1)

            def turn_pooled(g, par):
                pe.wait_ge(pooled_ready, g + 1)
                if not (isinstance(g, int) and g == 0):
                    pe.wait_ge(pooled_copied, g)
                pe.nop(nofuse=True)
                for c in range(GB):
                    pe.transpose(bank[c // 4][:, (c % 4) * P:(c % 4 + 1) * P], pooled[par][:, c, :], ident[:, :])
                pe.transpose(bank[2][0:2 * GB, 0:P], share[par][:, :, :].rearrange("p c k -> p (c k)"),
                             ident[:, :]).then_inc(pooled_turned, 1)

            def project(g, par):
                pe.wait_ge(pooled_copied, g + 1)
                pe.wait_ge(y_used, g + 1)
                for c in range(GB):
                    to = bank[4 + 2 * par + c // 4][:, (c % 4) * P:(c % 4 + 1) * P]
                    pe.matmul(to, lhsT=pooled_t[par][:, c, :], rhs=wc_t[:, :], start=True, stop=False)
                    last = pe.matmul(to, lhsT=share_t[par], rhs=bias_of[:, c, :], start=False, stop=True)
                last.then_inc(y_ready, 1)

            turn_pooled(0, 0)
            turn_pooled(1, 1)
            with pe.Fori(0, GROUPS // 2 - 1) as j:
                for par in range(2):
                    project(2 * j + par, par)
                    turn_pooled(2 * j + (par + 2), par)
            project(GROUPS - 2, 0)
            project(GROUPS - 1, 1)

        @block.vector
        def _(dve):
            dve.memset(zero_key[:, :], 0).then_inc(zero_ready, 1)
            dve.memset(turn_a[:, MAIN_COLS:EDGE_COLS], as_float(0x7FFF0000))
            dve.memset(turn_b[:, MAIN_COLS:EDGE_COLS], 0.0)
            dve.drain().then_inc(blank_ready, 1)
            dve.memset(rows_a[:, :], as_float(LAST_KEY))
            dve.memset(ones[:, :], 1.0)
            dve.memset(eps_col[:, :], 1e-5)
            dve.memset(carry[:, :], NEG)
            dve.wait_ge(iotas_ready, 1)
            dve.tensor_copy(iota_row[:, :], iota_i[:, :])
            dve.tensor_copy(part_idx[:, :], part_idx_i[:, :])
            dve.tensor_scalar(diag_eq[:, :, :], diag_i[:, :, :], 0.0, None, ALU.is_equal)
            dve.tensor_scalar(padkey_i[:, :], padkey_i[:, :], BLOCK_SHIFT, KEY_BASE | PAD_PLACE << DST_BITS,
                              ALU.logical_shift_left, ALU.bitwise_or)
            dve.tensor_scalar(bias_at[:, :, :], bias_at_i[:, :, :], 0.0, None, ALU.is_equal)
            dve.memset(bit_i[:, 0:1], 1)
            dve.drain()
            dve.tensor_scalar(ident[:, :], iota_row[:, :], part_idx[:, 0:1], None, ALU.is_equal)
            dve.tensor_reduce(same_col[:, :], diag_eq[:, :, :], AX.X, ALU.add)
            dve.tensor_reduce(is_lo[:, :], diag_eq[:, :, :].rearrange("p k l -> p l k"), AX.X, ALU.add)
            for k in range(LOG_ROWS):
                dve.tensor_scalar(bit_i[:, k + 1:k + 2], part_idx_i[:, :], k, 1, ALU.logical_shift_right, ALU.bitwise_and)
            dve.drain()
            dve.tensor_scalar(signs[:, :], bit_i[:, :], 2.0, -1.0, ALU.mult, ALU.add)
            dve.drain().then_inc(consts_ready, 1)
            dve.tensor_tensor(flips[:, :], signs[:, 1:], signs[:, 0:LOG_ROWS], ALU.mult)

            e = slice(0, P), slice(0, EDGE_COLS)
            dve.wait_ge(src_loaded, 32)
            dve.tensor_scalar(part_i[e], src_i[e], P - 1, DST_BITS, ALU.bitwise_and, ALU.logical_shift_left)
            dve.tensor_scalar(part2_i, src_i[e], 7, BLOCK_SHIFT, ALU.logical_shift_right, ALU.logical_shift_left)
            dve.drain()
            dve.scalar_tensor_tensor(part_i[e], part_i[e], KEY_BASE, part2_i, ALU.bitwise_or, ALU.bitwise_or)
            dve.drain()
            dve.wait_ge(dst_loaded, 32)
            keys_i = rows_a.ap().bitcast(I32)
            for here in ((slice(0, P), slice(0, MAIN_COLS)), (slice(0, REST_ROWS), slice(MAIN_COLS, PAD_AT))):
                dve.tensor_tensor(keys_i[here], part_i[here], dst_i[here], ALU.bitwise_or)
            dve.drain()
            dve.tensor_scalar(part_i[e], src_i[e], 7, LO - 1, ALU.logical_shift_right, ALU.bitwise_and)
            dve.tensor_scalar(part2_i, src_i[e], 11, None, ALU.logical_shift_right)
            dve.drain()
            lo_b, hi_b = (lohi_b[:, k * EDGE_COLS:(k + 1) * EDGE_COLS].rearrange("p (g k) -> p g k", k=HCOLS) for k in range(2))
            dve.tensor_copy(lo_b, part_i[e].rearrange("p (g k) -> p g k", k=HCOLS))
            dve.tensor_copy(hi_b, part2_i.rearrange("p (g k) -> p g k", k=HCOLS))
            dve.drain()
            for c in range(LO):
                dve.tensor_scalar(onehot[:, :, c, :], lo_b, float(c), None, ALU.is_equal)
            for c in range(HI):
                dve.tensor_scalar(onehot[:, :, LO + c, :], hi_b, float(c), None, ALU.is_equal)
            dve.drain().then_inc(onehots_ready, 1)
            rows, turns = (rows_a, rows_b), (turn_a, turn_b)
            done = [0, 0]

            def after_last(g):
                if done[g]:
                    dve.wait_ge(steps_done[g], done[g])

            def step_ends(g, ins):
                ins.then_inc(steps_done[g], 1)
                done[g] += 1

            def exchange_both_ways(g, a, b, s, k):
                form = dict(d=2, b=1 << (k - s - 1), t=2, j=1 << s)
                va, vb = (v[:, cols_of(g)].rearrange("p (a d b t j) -> p a d b t j", **form) for v in (a, b))
                after_last(g)
                for d in range(2):
                    lo, hi = va[:, :, d, :, 0, :], va[:, :, d, :, 1, :]
                    dve.tensor_tensor(vb[:, :, d, :, 0, :], lo, hi, ALU.min if d else ALU.max)
                    ins = dve.tensor_tensor(vb[:, :, d, :, 1, :], lo, hi, ALU.max if d else ALU.min)
                step_ends(g, ins)

            def exchange(g, a, b, s):
                va, vb = (v[:, cols_of(g)].rearrange("p (a t j) -> p a t j", t=2, j=1 << s) for v in (a, b))
                after_last(g)
                dve.tensor_tensor(vb[:, :, 0, :], va[:, :, 0, :], va[:, :, 1, :], ALU.min)
                step_ends(g, dve.tensor_tensor(vb[:, :, 1, :], va[:, :, 0, :], va[:, :, 1, :], ALU.max))

            def exchange_big(g, a, b, s):
                va, vb = (v[:, :].rearrange("p (b c) -> p b c", c=BCOLS) for v in (a, b))
                after_last(g)
                blocks = range(*PARTS[g])
                for n in blocks:
                    mate = n + (1 << s)
                    if not n >> s & 1 and mate < BIG:
                        dve.tensor_tensor(vb[:, n, :], va[:, n, :], va[:, mate, :], ALU.min)
                        ins = dve.tensor_tensor(vb[:, mate, :], va[:, n, :], va[:, mate, :], ALU.max)
                    elif not n >> s & 1:
                        ins = dve.tensor_copy(vb[:, n, :], va[:, n, :])
                step_ends(g, ins)

            def sign_of(k, n):
                return 1 if k == LOG_KEYS or n >> (k - LOG_BIG) & 1 else -1

            def set_signs(g, k):
                after_last(g)
                if k < LOG_BIG:
                    c = k - LOG_COLS
                    ins = dve.tensor_scalar(rows_a[:, cols_of(g)], rows_a[:, cols_of(g)], flips[:, c:c + 1], None, ALU.mult)
                elif k == LOG_BIG:
                    for n in range(*PARTS[g]):
                        here = rows_a[:, n * BCOLS:(n + 1) * BCOLS]
                        ins = dve.tensor_scalar(here, here, signs[:, LOG_ROWS:], float(sign_of(k, n)), ALU.mult, ALU.mult)
                else:
                    for n in range(*PARTS[g]):
                        if sign_of(k, n) != sign_of(k - 1, n):
                            here = rows_a[:, n * BCOLS:(n + 1) * BCOLS]
                            ins = dve.tensor_scalar(here, here, -1.0, None, ALU.mult)
                step_ends(g, ins)

            def short_phases(g):
                n = 0
                for k in range(1, LOG_COLS):
                    for s in reversed(range(k)):
                        exchange_both_ways(g, rows[n % 2], rows[1 - n % 2], s, k)
                        n += 1
                assert n % 2 == 0

            def by_turns(steps, step):
                for n in range(steps + LAG):
                    if n < steps:
                        step(0, n)
                    if n >= LAG:
                        step(1, n - LAG)

            short_phases(0)
            dve.wait_ge(hist_ready, 1)
            q = LO * HCOLS
            dve.tensor_tensor(hist_kept[:, :, :], hist_ps, same_col[:, :].unsqueeze(1).to_broadcast([q, HI, HCOLS]), ALU.mult)
            dve.drain()
            dve.tensor_reduce(hist_sum[:, :], hist_kept[:, :, :], AX.X, ALU.add)
            dve.drain()
            dve.tensor_tensor(hist_spread[:, :, :], hist_sum[:, :].unsqueeze(2).to_broadcast([q, HI, LO]),
                              is_lo[:, :].unsqueeze(1).to_broadcast([q, HI, LO]), ALU.mult).then_inc(spread_ready, 1)
            dve.wait_ge(counts_ready, 1)
            dve.tensor_scalar(padn_i[:, :], count_ps[:, 0:BLOCKS], -1.0, None, ALU.mult)
            dve.drain()
            dve.tensor_scalar(padn_j[:, :], padn_i[:, :], P - 1, None, ALU.bitwise_and)
            dve.drain()
            dve.tensor_scalar(pad_off[:, :], padn_j[:, :], part_idx[:, 0:1], as_float(LAST_KEY), ALU.is_le, ALU.mult)
            dve.drain()
            dve.tensor_tensor(rows_a[:, PAD_AT:PAD_AT + BLOCKS], padkey_i.ap().bitcast(F32), pad_off[:, :], ALU.max)
            dve.drain()

            short_phases(1)
            for k in range(LOG_COLS, LOG_KEYS + 1):
                if k == LOG_KEYS:
                    set_signs(0, k)
                    for g in range(2):
                        after_last(g)
                    for n in range(BIG - 4):
                        a0, a1, b0, b1 = (v[:, m * BCOLS:(m + 1) * BCOLS] for v in (rows_a, rows_b) for m in (n, n + 4))
                        dve.tensor_tensor(b0, a0, a1, ALU.min)
                        dve.tensor_tensor(b1, a0, a1, ALU.max)
                    alone = slice((BIG - 4) * BCOLS, 4 * BCOLS)
                    step_ends(0, dve.tensor_copy(rows_b[:, alone], rows_a[:, alone]))
                    dve.drain().then_inc(steps_done[1], 2)
                    done[1] += 2
                    big_from = 1
                else:
                    for g in range(2):
                        set_signs(g, k)
                    big_from = 0
                big = list(reversed(range(max(0, k - LOG_BIG))))
                for n in range(big_from, len(big)):
                    for g in range(2):
                        exchange_big(g, rows[n % 2], rows[1 - n % 2], big[n])

                def step_in_turned(g, n):
                    if n == 0:
                        dve.wait_ge(turn_copied[g], 4 * (k - LOG_COLS - 1) + 2)
                    exchange(g, turns[n % 2], turns[1 - n % 2], min(k - LOG_COLS, LOG_ROWS) - 1 - n)

                def step_in_rows(g, n):
                    if n == 0 and k > LOG_COLS:
                        dve.wait_ge(turn_copied[g], 4 * (k - LOG_COLS - 1) + 4)
                    exchange(g, rows[n % 2], rows[1 - n % 2], LOG_COLS - 1 - n)

                by_turns(min(k - LOG_COLS, LOG_ROWS), step_in_turned)
                by_turns(LOG_COLS, step_in_rows)
            assert done == [all_steps, all_steps]
            dve.drain()
            dve.wait_ge(table_stored, 16)
            dve.memset(sums, 0.0)
            for k in range(2):
                dve.memset(share[k][:, :, 1:2], 1.0)
            dve.drain().then_inc(sums_added, 2 * BATCH)

            def prepare(i, j_uses, par):
                dve.wait_ge(k3_loaded[par], j_uses * 48 + 48)
                own = k3[par][:, 1, :]
                dve.tensor_scalar(node_i[:, :, :], k3[par][:, :, :], DST_BITS, None, ALU.logical_shift_right)
                dve.tensor_scalar(dst_r[:, :], own, DST_MASK, None, ALU.bitwise_and)
                dve.tensor_scalar(place_r[:, :], own, DST_BITS, PLACE_MASK, ALU.logical_shift_right, ALU.bitwise_and)
                dve.tensor_scalar(prev_place_i[:, :], k3[par][:, 0, 0:1], DST_BITS, PLACE_MASK, ALU.logical_shift_right, ALU.bitwise_and)
                dve.tensor_scalar(block_i[:, :], k3[par][:, 1, 0:1], BLOCK_SHIFT, 127, ALU.logical_shift_right, ALU.bitwise_and)
                dve.drain().then_inc(k3_used, 1)
                if not (isinstance(i, int) and i == 0):
                    dve.wait_ge(prep_turned, i)
                dve.tensor_copy(node_f[:, :, :], node_i[:, :, :])
                dve.tensor_copy(dst_f[:, :], dst_r[:, :])
                dve.tensor_copy(place_f[:, :], place_r[:, :])
                dve.tensor_copy(prev_place[par][:, :], prev_place_i[:, :])
                dve.tensor_scalar(sums_at[:, :], block_i[:, :], float(WIDTH), None, ALU.mult)
                dve.drain()
                dve.tensor_scalar(pen_tile[par][:, :], node_f[:, 1, :], node_f[:, 0, 0:1], NEG, ALU.not_equal, ALU.mult)
                dve.tensor_tensor(differs[:, :, :], node_f[:, 1:2, :].to_broadcast([T, 2, P]), node_f[:, 0:3:2, :], ALU.not_equal)
                dve.drain()
                dve.tensor_scalar(pen[par][:, :, :], differs[:, :, :], NEG, None, ALU.mult)
                dve.tensor_scalar(goes_on[par][:, :], pen_tile[par][:, 0:1], 0.0, None, ALU.is_equal)
                dve.drain().then_inc(prep_done, 1)

            def softmax(i, par):
                dve.wait_ge(gates_turned, i + 1)
                dve.tensor_tensor_scan(run_max[:, :], pen[par][:, 0, :], gate_rows, NEG, ALU.add, ALU.max)
                dve.drain().then_inc(run_max_done, 1)
                dve.wait_ge(tile_max_turned, i + 1)
                dve.tensor_tensor_scan(carry[0:1, 1:T + 1], tile_pen[par][:, :], tile_max_ps, carry[0:1, 0:1], ALU.add, ALU.max)
                dve.drain().then_inc(carry_done, 1)
                dve.wait_ge(carry_turned, i + 1)
                dve.tensor_copy(carry_col[:, :], carry_ps)
                dve.tensor_copy(carry[0:1, 0:1], carry[0:1, T:T + 1])
                dve.drain()
                dve.scalar_tensor_tensor(run_max2[:, :], pen_tile[par][:, :], carry_col[:, 0:1], run_max[:, :], ALU.add, ALU.max)
                dve.drain()
                dve.tensor_tensor_scan(seg_max[:, ::-1], pen[par][:, 1, ::-1], run_max2[:, ::-1], NEG, ALU.add, ALU.max)
                dve.drain()
                dve.tensor_tensor(expo[:, 0, :], gate_rows, seg_max[:, :], ALU.subtract)
                dve.scalar_tensor_tensor(drop[:, :], carry_col[:, :], seg_max[:, 0:1], goes_on[par][:, :], ALU.subtract, ALU.mult)
                dve.drain()
                dve.tensor_scalar(expo[:, 1, :], iota_row[0:T, :], prev_place[par][:, 0:1], drop[:, 0:1], ALU.is_equal, ALU.mult)
                dve.drain().then_inc(expo_done, 1)

            def add_batch(i, par, b, at_cols):
                dve.wait_ge(tiles_summed, i * NB + (b + 1))
                for u in range(BATCH):
                    t = b * BATCH + u
                    here = sums[:, bass.ds(at_cols[t], WIDTH)]
                    dve.wait_ge(sums_added, i * T + (t + 2 * BATCH))
                    dve.scalar_tensor_tensor(here, here, weights[par][:, 1, t:t + 1], tile_ps((b % 2) * BATCH + u),
                                             ALU.mult, ALU.add).then_inc(sums_added, 1)

            prepare(0, 0, 0)
            with loop(ENGINE.DVE, 0, CHUNKS // 2) as j:
                for par in range(2):
                    i = 2 * j + par
                    prepare(i + 1, j + par, 1 - par)
                    softmax(i, par)
                    dve.wait_ge(weights_ready, i + 1)
                    dve.wait_ge(prep_copied, i + 1)
                    dve.nop(nofuse=True)
                    at_cols = {}
                    for b in range(NB):
                        if b % 2 == 0:
                            n = 2 * BATCH if b + 1 < NB else BATCH
                            got = nc.values_load_multi_w_load_instructions(
                                offs[par][0:1, b * BATCH:b * BATCH + n], engines=[mybir.EngineType.DVE], min_val=0,
                                max_val=(BLOCKS - 1) * WIDTH, skip_runtime_bounds_check_because="a block times the width")[1]
                            new_cols = {b * BATCH + m: got[m] for m in range(n)}
                        for u in range(BATCH):
                            t = b * BATCH + u
                            ins = dve.tensor_scalar(spread[:, (b % 2) * BATCH + u, :], iota_row[:, :], place_t[par][:, t:t + 1],
                                                    weights[par][:, 0, t:t + 1], ALU.is_equal, ALU.mult)
                        ins.then_inc(spread_done, 1)
                        if b > 0:
                            add_batch(i, par, b - 1, at_cols)
                        at_cols.update(new_cols)
                    add_batch(i, par, NB - 1, at_cols)

            def pool_group(g, par):
                here = sums[:, bass.ds(g * GB * WIDTH, GB * WIDTH)].rearrange("p (c w) -> p c w", w=WIDTH)
                dve.drain()
                dve.tensor_scalar(den[:, :], here[:, :, FEAT], 1e-16, None, ALU.add)
                dve.drain()
                dve.reciprocal(den[:, :], den[:, :])
                dve.drain()
                if not (isinstance(g, int) and g < 2):
                    dve.wait_ge(pooled_turned, g - 1)
                dve.tensor_tensor(share[par][:, :, 0], here[:, :, FEAT], den[:, :], ALU.mult)
                dve.tensor_tensor(pooled[par][:, :, :], here[:, :, 0:FEAT], den[:, :].unsqueeze(2).to_broadcast([P, GB, FEAT]),
                                  ALU.mult).then_inc(pooled_ready, 1)

            def add_and_measure(g, par, x_count, outs):
                dve.wait_ge(x_in[par], x_count)
                dve.wait_ge(y_ready, g + 1)
                if outs is not None:
                    dve.wait_ge(out_ready, outs)
                for c, n in ((0, 4), (4, GB - 4)):
                    ps = bank[4 + 2 * par + c // 4][:, 0:n * P].rearrange("p (c f) -> p c f", f=P)
                    dve.tensor_tensor(resid[par][:, c:c + n, :], ps, x_grp[par][:, c:c + n, :], ALU.add)
                dve.drain().then_inc(y_used, 1)
                for c in range(GB):
                    dve.bn_stats(stats[:, c, :], resid[par][:, c, :])
                dve.drain()
                for c in range(GB):
                    dve.bn_aggr(mean_var[par][:, c, :], stats[:, c, :])
                dve.drain().then_inc(var_ready, 1)

            def scale_and_shift(g, par):
                dve.wait_ge(std_ready, g + 1)
                dve.reciprocal(inv_std[par][:, :], std[par][:, :])
                dve.drain()
                dve.scalar_tensor_tensor(shift[par][:, :], mean_var[par][:, :, 0], -1.0, inv_std[par][:, :], ALU.mult, ALU.mult)
                dve.drain().then_inc(norm_ready, 1)

            dve.drain().then_inc(y_used, 2)
            def step(g, par, x_count, outs, more=True):
                add_and_measure(g, par, x_count, outs)
                scale_and_shift(g, par)
                if more:
                    pool_group(g + 3, 1 - par)

            for g in range(3):
                pool_group(g, g % 2)
            step(0, 0, 16, None)
            step(1, 1, 16, None)
            with dve.Fori(1, GROUPS // 2 - 2) as j:
                step(2 * j, 0, 16 * j + 16, 2 * j - 1)
                step(2 * j + 1, 1, 16 * j + 16, 2 * j)
            step(GROUPS - 4, 0, 16 * (GROUPS // 2 - 1), GROUPS - 5)
            step(GROUPS - 3, 1, 16 * (GROUPS // 2 - 1), GROUPS - 4, more=False)
            step(GROUPS - 2, 0, 16 * (GROUPS // 2), GROUPS - 3, more=False)
            step(GROUPS - 1, 1, 16 * (GROUPS // 2 + 1), GROUPS - 2, more=False)


_INS = ['x', 'src', 'dst', 'L0_gnn_W_lin', 'L0_gnn_b_lin', 'L0_gnn_W_gate', 'L0_gnn_b_gate', 'L0_gnn_W_out', 'L0_gnn_b_out']


def kernel(**inputs):
    import concourse.bacc as bacc
    from concourse.bass_utils import run_bass_kernel_spmd as run
    nc = bacc.Bacc("TRN2", target_bir_lowering=False, num_devices=1)
    arrays, args = {}, []
    for name in _INS:
        a = np.ascontiguousarray(inputs[name])
        arrays[f"in_{name}"] = a
        args.append(nc.dram_tensor(f"in_{name}", a.shape, mybir.dt.from_np(a.dtype), kind="ExternalInput").ap())
    out = nc.dram_tensor("out_0", (NODES, FEAT), F32, kind="ExternalOutput").ap()
    graph_attention(nc, *args, out)
    r = run(nc, [arrays], core_ids=[0])
    return r.results[0]["out_0"]
```

```python
import numpy as np
import concourse.bass as bass
from concourse import mybir
from contextlib import ExitStack

F32 = mybir.dt.float32
BF16 = mybir.dt.bfloat16
I32 = mybir.dt.int32
ALU = mybir.AluOpType
ACT = mybir.ActivationFunctionType
AX = mybir.AxisListType
ENGINE = mybir.EngineType

P = 128
NODES, FEAT, EDGES = 12500, 128, 212500
BLOCKS = -(-NODES // P)
LAST_ROWS = NODES - (BLOCKS - 1) * P

DST_BITS, PLACE_BITS = 14, 8
BLOCK_SHIFT = DST_BITS + PLACE_BITS
KEY_BASE = 0x40000000
PAD_PLACE = 255
DST_MASK, PLACE_MASK = (1 << DST_BITS) - 1, (1 << PLACE_BITS) - 1
LAST_KEY = KEY_BASE | (BLOCKS - 1) << BLOCK_SHIFT | PAD_PLACE << DST_BITS

LOG_COLS, LOG_ROWS = 8, 7
BIG = 7
LOG_BIG = LOG_COLS + LOG_ROWS
LOG_KEYS = LOG_BIG + 3
BCOLS = 1 << LOG_COLS
COLS = BIG * BCOLS
KEYS = P * COLS
HALF = COLS // 2
BANK = 512
PARTS = [(0, 4), (4, 7)]
LAG = 2

MAIN_COLS = 1656
REST_ROWS, REST_COLS = 14, 38
PAD_AT = MAIN_COLS + REST_COLS
TAIL_ROWS = 16

LO, HI, HCOLS = 16, 7, 4
EDGE_COLS = 1696
HGROUPS = EDGE_COLS // HCOLS

T = 40
CHUNKS = 44
TILES = (EDGES + BLOCKS * (P - 1)) // P
BATCH = 4
NB = T // BATCH
EARLY = 4 * BATCH
WIDTH = FEAT + 1
ROW = FEAT + 2
NODE_ROWS, NODE_COLS = 125, 100
GATE_COLS = 10
NEG = -1.0e30

GB = 7
GROUPS = BLOCKS // GB


def check_shapes():
    assert P * MAIN_COLS + REST_ROWS * REST_COLS == EDGES and NODE_ROWS * NODE_COLS == NODES
    assert EARLY % BATCH == 0 and CHUNKS % 4 == 0 and (CHUNKS - 1) * T + EARLY < TILES <= CHUNKS * T and (CHUNKS + 1) * T * P < KEYS + TAIL_ROWS * P
    assert PAD_AT + BLOCKS <= COLS and PAD_AT <= EDGE_COLS <= COLS and PARTS[1][0] * BCOLS <= MAIN_COLS and HALF >= GB * FEAT and GB == 7
    assert LO * HI >= BLOCKS and BLOCKS % GB == 0 and GROUPS % 2 == 0


def as_float(bits):
    return float(np.array([bits], np.uint32).view(np.float32)[0])


def graph_attention(nc, x, src, dst, w_lin, b_lin, w_gate, b_gate, w_out, b_out, out):
    check_shapes()
    with ExitStack() as ctx:
        def sb(name, shape, dt=F32):
            return ctx.enter_context(nc.sbuf_tensor(name, shape, dt))

        def sem(name):
            return ctx.enter_context(nc.semaphore(name))

        table = nc.dram_tensor("node_table", (NODES, ROW), F32).ap()
        skeys = nc.dram_tensor("sorted_keys", (1 + KEYS + TAIL_ROWS * P,), I32).ap()

        rows_a, rows_b = sb("rows_a", [P, COLS]), sb("rows_b", [P, COLS])
        turn_a, turn_b = sb("turn_a", [P, COLS]), sb("turn_b", [P, COLS])
        src_i, dst_i = turn_a.ap().bitcast(I32), turn_b.ap().bitcast(I32)
        part_i = rows_b.ap().bitcast(I32)
        lohi_b = turn_b.ap().bitcast(BF16)
        nodes_sb = sb("nodes_sb", [P, 13000])
        node_rows = nodes_sb[0:NODE_ROWS, 0:NODE_COLS * ROW].rearrange("p (n f) -> p n f", f=ROW)
        sums = nodes_sb[:, 0:BLOCKS * WIDTH]
        arena = sb("arena", [P, 23 * EDGE_COLS // 2 + EDGE_COLS])
        onehot = arena[:, 0:23 * EDGE_COLS // 2].bitcast(BF16).rearrange("p (g c k) -> p g c k", c=LO + HI, k=HCOLS)
        part2_i = arena[:, 23 * EDGE_COLS // 2:23 * EDGE_COLS // 2 + EDGE_COLS].bitcast(I32)
        gathered_rows = [arena[:, k * T * ROW:(k + 1) * T * ROW].rearrange("p (t f) -> p t f", f=ROW) for k in range(2)]
        gate_prod = sb("gate_prod", [P, GATE_COLS, FEAT])
        gate_junk = sb("gate_junk", [P, FEAT])
        gate_sum = sb("gate_sum", [P, NODE_COLS])
        wg = sb("wg", [P, FEAT])
        bg = sb("bg", [P, 1])

        iota_i, iota_row = sb("iota_i", [P, P], I32), sb("iota_row", [P, P])
        part_idx_i, part_idx = sb("part_idx_i", [P, 1], I32), sb("part_idx", [P, 1])
        ident = sb("ident", [P, P])
        ones = sb("ones", [P, P])
        diag_i = sb("diag_i", [LO * HCOLS, HCOLS, LO], I32)
        diag_eq = sb("diag_eq", [LO * HCOLS, HCOLS, LO])
        same_col = sb("same_col", [LO * HCOLS, HCOLS])
        is_lo = sb("is_lo", [LO * HCOLS, LO])
        hist_kept = sb("hist_kept", [LO * HCOLS, HI, HCOLS])
        hist_sum = sb("hist_sum", [LO * HCOLS, HI])
        hist_spread = sb("hist_spread", [LO * HCOLS, HI, LO])
        padkey_i = sb("padkey_i", [P, BLOCKS], I32)
        padn_i = sb("padn_i", [P, BLOCKS], I32)
        padn_j = sb("padn_j", [P, BLOCKS], I32)
        pad_off = sb("pad_off", [P, BLOCKS])
        bit_i = sb("bit_i", [P, LOG_ROWS + 1], I32)
        signs = sb("signs", [P, LOG_ROWS + 1])
        flips = sb("flips", [P, LOG_ROWS])

        wl_sb, wo_sb, wo_t = sb("wl_sb", [P, P]), sb("wo_sb", [P, P]), sb("wo_t", [P, P])
        bl_col = sb("bl_col", [P, 1])
        wc_t = sb("wc_t", [P, P])
        bias2 = sb("bias2", [2, P])
        zero_key = sb("zero_key", [1, 1], I32)
        eps_col = sb("eps_col", [P, 1])

        k3 = [sb(f"k3_{k}", [T, 3, P], I32) for k in range(2)]
        node_i, node_f = sb("node_i", [T, 3, P], I32), sb("node_f", [T, 3, P])
        dst_r, place_r = sb("dst_r", [T, P], I32), sb("place_r", [T, P], I32)
        prev_place_i, block_i = sb("prev_place_i", [T, 1], I32), sb("block_i", [T, 1], I32)
        dst_f, place_f = sb("dst_f", [T, P]), sb("place_f", [T, P])
        prev_place = [sb(f"prev_place{k}", [T, 1]) for k in range(2)]
        sums_at = sb("sums_at", [T, 1])
        differs = sb("differs", [T, 2, P])
        pen = [sb(f"pen{k}", [T, 2, P]) for k in range(2)]
        pen_tile = [sb(f"pen_tile{k}", [T, P]) for k in range(2)]
        goes_on = [sb(f"goes_on{k}", [T, 1]) for k in range(2)]
        gather_at = [sb(f"gather_at{k}", [P, T], I32) for k in range(2)]
        place_t = [sb(f"place_t{k}", [P, T]) for k in range(2)]
        offs = [sb(f"offs{k}", [1, T], I32) for k in range(2)]
        tile_pen = [sb(f"tile_pen{k}", [1, T]) for k in range(2)]
        run_max, run_max2, seg_max = sb("run_max", [T, P]), sb("run_max2", [T, P]), sb("seg_max", [T, P])
        carry = sb("carry", [1, T + 1])
        carry_col = sb("carry_col", [T, 1])
        drop = sb("drop", [T, 1])
        expo = sb("expo", [T, 2, P])
        weights = [sb(f"weights{k}", [P, 2, T]) for k in range(2)]
        spread = sb("spread", [P, 2 * BATCH, P])

        def again(buf, k, width):
            return buf[:, k * HALF:k * HALF + GB * width].rearrange("p (c f) -> p c f", f=width)

        x_grp, y_grp, pooled = ([again(buf, k, FEAT) for k in range(2)] for buf in (rows_a, rows_b, turn_a))
        resid = [again(turn_b, k, FEAT) for k in range(2)]
        pooled_t = [arena[:, k * HALF:k * HALF + GB * P].rearrange("p (c f) -> p c f", f=P) for k in range(2)]
        free_at = 2 * T * ROW
        inv_den = arena[:, free_at:free_at + BLOCKS]
        ratio = arena[:, free_at + BLOCKS:free_at + 2 * BLOCKS]
        share = arena[:, free_at + 2 * BLOCKS:free_at + 8 * BLOCKS].rearrange("p (b k) -> p b k", k=6)
        share_t = [sb(f"share_t{k}", [6 * GB, P], BF16) for k in range(2)]
        bias_at_i, bias_at = (arena[0:2, free_at + (8 + k * 9) * BLOCKS:free_at + (17 + k * 9) * BLOCKS].bitcast(dt)
                              .rearrange("p (g k r) -> p g k r", k=3, r=6 * GB) for k, dt in ((0, I32), (1, F32)))
        bias_parts = sb("bias_parts", [2, 3, P])
        bias_part_b = sb("bias_part_b", [2, P], BF16)
        bias_left = sb("bias_left", [2, 2, P])
        bias_of = sb("bias_of", [6 * GB, GB, P], BF16)
        stats = sb("stats", [P, GB, 6])
        mean_var = [sb(f"mean_var{k}", [P, GB, 2]) for k in range(2)]
        std, inv_std, shift = ([sb(f"{name}{k}", [P, GB]) for k in range(2)] for name in ("std", "inv_std", "shift"))

        bank = [ctx.enter_context(nc.psum_tensor(f"bank{k}", [P, 512], F32)) for k in range(8)]
        hist_ps = bank[7][0:LO * HCOLS, 0:HI * HCOLS].rearrange("p (h k) -> p h k", k=HCOLS)
        count_ps = bank[6][:, 0:HI * LO]
        gate_rows = bank[4][0:T, 0:P]
        tile_block_ps, tile_pen_ps, tile_max_ps = bank[6][0:1, 256:256 + T], bank[6][0:1, 384:384 + T], bank[5][0:1, 128:128 + T]
        carry_ps = bank[5][0:T, 192:193]
        prep_ps = bank[6][:, 0:2 * T].rearrange("p (a t) -> p a t", a=2)
        expo_ps = bank[7][:, 0:2 * T].rearrange("p (a t) -> p a t", a=2)

        def tile_ps(slot):
            return bank[slot // 2][:, (slot % 2) * 256:(slot % 2) * 256 + WIDTH]

        src_loaded, dst_loaded, x_loaded, weights_loaded = sem("src_loaded"), sem("dst_loaded"), sem("x_loaded"), sem("weights_loaded")
        iotas_ready, consts_ready = sem("iotas_ready"), sem("consts_ready")
        prod_ready, prod_used, gates_ready, ones_ready = sem("prod_ready"), sem("prod_used"), sem("gates_ready"), sem("ones_ready")
        table_stored, keys_stored, zero_ready = sem("table_stored"), sem("keys_stored"), sem("zero_ready")
        onehots_ready, hist_ready, spread_ready, counts_ready = sem("onehots_ready"), sem("hist_ready"), sem("spread_ready"), sem("counts_ready")
        wo_turned, wo_copied, wc_ready, wc_copied = sem("wo_turned"), sem("wo_copied"), sem("wc_ready"), sem("wc_copied")
        bias_iota_ready, bias_split, bias_spread, bias_copied = sem("bias_iota_ready"), sem("bias_split"), sem("bias_spread"), sem("bias_copied")
        steps_done, turned, turn_copied = ([sem(f"{name}{g}") for g in range(2)] for name in ("steps_done", "turned", "turn_copied"))
        part_stored = [sem(f"part_stored{g}") for g in range(2)]
        blank_ready, sums_blank = sem("blank_ready"), sem("sums_blank")
        k3_loaded = [sem(f"k3_loaded{k}") for k in range(2)]
        k3_used = sem("k3_used")
        prep_done, prep_turned, prep_copied = sem("prep_done"), sem("prep_turned"), sem("prep_copied")
        rows_gathered = [sem(f"rows_gathered{k}") for k in range(2)]
        gather_buf_free, late_gathered = sem("gather_buf_free"), sem("late_gathered")
        gates_turned, run_max_done, tile_max_turned, carry_done, carry_turned = (
            sem("gates_turned"), sem("run_max_done"), sem("tile_max_turned"), sem("carry_done"), sem("carry_turned"))
        expo_done, expo_turned, weights_ready = sem("expo_done"), sem("expo_turned"), sem("weights_ready")
        spread_done, tiles_summed, sums_added = sem("spread_done"), sem("tiles_summed"), sem("sums_added")
        x_in = [sem(f"x_in{k}") for k in range(2)]
        dens_ready, pooled_ready, pooled_turned, pooled_copied, y_ready, y_used = (
            sem("dens_ready"), sem("pooled_ready"), sem("pooled_turned"), sem("pooled_copied"), sem("y_ready"), sem("y_used"))
        var_ready, std_ready, norm_ready, out_ready = sem("var_ready"), sem("std_ready"), sem("norm_ready"), sem("out_ready")
        normalised, share_ready = sem("normalised"), sem("share_ready")
        stored = [sem(f"stored{k}") for k in range(2)]

        to_cols, to_rows = {}, {}
        steps = LOG_COLS * (LOG_COLS - 1) // 2
        for k in range(LOG_COLS, LOG_KEYS + 1):
            steps += 1 + max(0, k - LOG_BIG)
            to_cols[k] = steps
            steps += min(k - LOG_COLS, LOG_ROWS)
            to_rows[k] = steps
            steps += LOG_COLS
        all_steps = steps
        turning = [(k, back, g, at[k]) for k in range(LOG_COLS + 1, LOG_KEYS + 1) for back, at in enumerate((to_cols, to_rows)) for g in range(2)]

        def cols_of(g):
            return slice(PARTS[g][0] * BCOLS, PARTS[g][1] * BCOLS)

        def banks_of(k, back, g):
            lo, hi = PARTS[g][0] * BCOLS, PARTS[g][1] * BCOLS
            for n in range(2):
                at = lo + n * BANK
                yield bank[4 * back + 2 * g + n], at, min(BANK, hi - at), 4 * (k - LOG_COLS - 1) + 2 * back + n + 1

        def loop(engine, start, end):
            return nc.Fori(start, end, engines=[engine], hint_back_edge=True)

        block = ctx.enter_context(nc.Block())

        def group_of(a, g, parts):
            if parts == "whole":
                return a[bass.ds(g * GB * P, GB * P), :].rearrange("(c p) f -> p c f", p=P)
            if parts == "full":
                return a[g * GB * P:g * GB * P + (GB - 1) * P, :].rearrange("(c p) f -> p c f", p=P)
            return a[NODES - LAST_ROWS:NODES, :]

        @block.sync
        def _(sp):
            main, rest = slice(0, P * MAIN_COLS), slice(P * MAIN_COLS, EDGES)
            sp.dma_start(src_i[:, 0:MAIN_COLS], src[main].rearrange("(p n) -> p n", n=MAIN_COLS)).then_inc(src_loaded, 16)
            sp.wait_ge(blank_ready, 1)
            sp.dma_start(src_i[0:REST_ROWS, MAIN_COLS:PAD_AT], src[rest].rearrange("(p n) -> p n", n=REST_COLS)).then_inc(src_loaded, 16)
            sp.dma_start(dst_i[:, 0:MAIN_COLS], dst[main].rearrange("(p n) -> p n", n=MAIN_COLS)).then_inc(dst_loaded, 16)
            sp.dma_start(dst_i[0:REST_ROWS, MAIN_COLS:PAD_AT], dst[rest].rearrange("(p n) -> p n", n=REST_COLS)).then_inc(dst_loaded, 16)
            sp.dma_start(node_rows[:, :, 0:FEAT], x.rearrange("(p n) f -> p n f", n=NODE_COLS)).then_inc(x_loaded, 16)
            sp.wait_ge(gates_ready, 1)
            sp.wait_ge(ones_ready, 1)
            sp.dma_start(table.rearrange("(p n) f -> p n f", n=NODE_COLS), node_rows).then_inc(table_stored, 16)
            sp.wait_ge(zero_ready, 1)
            sp.dma_start(skeys[0:1].rearrange("(a n) -> a n", a=1), zero_key[:, :]).then_inc(keys_stored, 16)
            sp.dma_start(skeys[1 + KEYS:].rearrange("(p n) -> p n", n=P), iota_i[0:TAIL_ROWS, :]).then_inc(keys_stored, 16)

            def store_keys(g):
                sp.wait_ge(steps_done[g], all_steps)
                lo, hi = PARTS[g]
                sp.dma_start(skeys[1 + lo * P * BCOLS:1 + hi * P * BCOLS].rearrange("(b p c) -> p b c", p=P, c=BCOLS),
                             rows_a.ap().bitcast(I32)[:, cols_of(g)].rearrange("p (b c) -> p b c", c=BCOLS)).then_inc(part_stored[g], 16)

            def load_chunk(i, par):
                for shift in range(3):
                    sp.dma_start(k3[par][:, shift, :],
                                 skeys[bass.ds(i * (T * P) + shift, T * P)].rearrange("(t n) -> t n", n=P)).then_inc(k3_loaded[par], 16)

            store_keys(0)
            sp.wait_ge(keys_stored, 32)
            sp.wait_ge(part_stored[0], 16)
            load_chunk(0, 0)
            store_keys(1)
            sp.wait_ge(part_stored[1], 16)
            with sp.Fori(0, CHUNKS // 2 - 1) as j:
                sp.wait_ge(k3_used, 2 * j + 1)
                load_chunk(2 * j + 1, 1)
                sp.wait_ge(k3_used, 2 * j + 2)
                load_chunk(2 * j + 2, 0)
            sp.wait_ge(k3_used, CHUNKS - 1)
            load_chunk(CHUNKS - 1, 1)

            def load_x(g, par, last=False):
                if last:
                    sp.dma_start(x_grp[par][:, 0:GB - 1, :], group_of(x, g, "full")).then_inc(x_in[par], 16)
                    sp.dma_start(x_grp[par][0:LAST_ROWS, GB - 1, :], group_of(x, g, "rest")).then_inc(x_in[par], 16)
                else:
                    sp.dma_start(x_grp[par][:, :, :], group_of(x, g, "whole")).then_inc(x_in[par], 16)

            def store(g, par, last=False):
                sp.wait_ge(out_ready, g + 1)
                if last:
                    sp.dma_start(group_of(out, g, "full"), y_grp[par][:, 0:GB - 1, :]).then_inc(stored[par], 16)
                    sp.dma_start(group_of(out, g, "rest"), y_grp[par][0:LAST_ROWS, GB - 1, :]).then_inc(stored[par], 16)
                else:
                    sp.dma_start(group_of(out, g, "whole"), y_grp[par][:, :, :]).then_inc(stored[par], 16)

            def step(g, par, last=False):
                sp.wait_ge(y_used, g + 3)
                load_x(g + 2, par, last)
                store(g, par)

            load_x(0, 0)
            load_x(1, 1)
            with sp.Fori(0, GROUPS // 2 - 2) as j:
                step(2 * j, 0)
                step(2 * j + 1, 1)
            step(GROUPS - 4, 0)
            step(GROUPS - 3, 1, last=True)
            store(GROUPS - 2, 0)
            store(GROUPS - 1, 1, last=True)
            sp.wait_ge(stored[0], 16 * (GROUPS // 2))
            sp.wait_ge(stored[1], 16 * (GROUPS // 2 + 1))
            sp.wait_ge(table_stored, 16)

        @block.gpsimd
        def _(pool):
            pool.iota(iota_i[:, :], [[1, P]], base=0, channel_multiplier=0)
            pool.iota(part_idx_i[:, :], [[1, 1]], base=0, channel_multiplier=1)
            pool.iota(padkey_i[:, :], [[1, BLOCKS]], base=0, channel_multiplier=0)
            pool.iota(diag_i[:, :, :], [[-1, HCOLS], [-HCOLS, LO]], base=0, channel_multiplier=1)
            pool.drain().then_inc(iotas_ready, 1)
            pool.wait_ge(x_loaded, 16)
            pool.wait_ge(weights_loaded, 16 * 6)
            pool.memset(node_rows[:, :, FEAT:FEAT + 1], 1.0).then_inc(ones_ready, 1)
            for c in range(NODE_COLS // GATE_COLS):
                if c > 0:
                    pool.wait_ge(prod_used, c)
                pool.tensor_tensor(gate_prod[0:NODE_ROWS], node_rows[:, c * GATE_COLS:(c + 1) * GATE_COLS, 0:FEAT],
                                   wg[0:NODE_ROWS].unsqueeze(1).to_broadcast([NODE_ROWS, GATE_COLS, FEAT]),
                                   ALU.mult).then_inc(prod_ready, 1)
            pool.wait_ge(table_stored, 16)
            pool.memset(sums, 0.0).then_inc(sums_blank, 1)
            pool.wait_ge(hist_ready, 1)
            pool.iota(bias_at_i[:, :, :, :], [[-6, GB], [-1, 3], [1, 6 * GB]], base=0, channel_multiplier=-3)
            pool.drain().then_inc(bias_iota_ready, 1)
            def gather(par, tiles, gathered):
                for t in tiles:
                    pool.indirect_dma_start(out=gathered_rows[par][:, t, :], out_offset=None, in_=table[:, :],
                                            in_offset=bass.IndirectOffsetOnAxis(ap=gather_at[par][:, t:t + 1], axis=0)
                                            ).then_inc(gathered, 16)

            def gather_chunks(j, last=False):
                for c in range(4):
                    par = c % 2
                    pool.wait_ge(prep_copied, 4 * j + (c + 1))
                    pool.wait_ge(gather_buf_free, 4 * j + (c + 1))
                    pool.nop(nofuse=True)
                    early = EARLY if last and c == 3 else T
                    gather(par, range(early), rows_gathered[par])
                    gather(par, range(early, TILES - (CHUNKS - 1) * T if last and c == 3 else T), late_gathered)

            with loop(ENGINE.Pool, 0, CHUNKS // 4 - 1) as j:
                gather_chunks(j)
            gather_chunks(CHUNKS // 4 - 1, last=True)

            def pool_group(g, par):
                if not (isinstance(g, int) and g < 2):
                    pool.wait_ge(pooled_turned, g - 1)
                here = sums[:, bass.ds(g * GB * WIDTH, GB * WIDTH)].rearrange("p (c w) -> p c w", w=WIDTH)
                pool.tensor_tensor(pooled[par][:, :, :], here[:, :, 0:FEAT],
                                   inv_den[:, bass.ds(g * GB, GB)].unsqueeze(2).to_broadcast([P, GB, FEAT]),
                                   ALU.mult).then_inc(pooled_ready, 1)

            pool.wait_ge(dens_ready, 1)
            pool_group(0, 0)
            pool_group(1, 1)
            with loop(ENGINE.Pool, 1, GROUPS // 2) as j:
                pool_group(2 * j, 0)
                pool_group(2 * j + 1, 1)

        @block.scalar
        def _(act):
            act.dma_start(wg[:, :], w_gate.partition_broadcast(P)).then_inc(weights_loaded, 16)
            act.dma_start(bg[:, :], b_gate.rearrange("(a n) -> a n", a=1).partition_broadcast(P)).then_inc(weights_loaded, 16)
            act.dma_start(wl_sb[:, :], w_lin).then_inc(weights_loaded, 16)
            act.dma_start(wo_sb[:, :], w_out).then_inc(weights_loaded, 16)
            act.dma_start(bl_col[:, :], b_lin.rearrange("(n a) -> n a", a=1)).then_inc(weights_loaded, 16)
            act.dma_start(bias2[1:2, :], b_out.rearrange("(a n) -> a n", a=1)).then_inc(weights_loaded, 16)
            act.wait_ge(wo_turned, 1)
            act.activation(wo_t[:, :], bank[4][:, 0:P], ACT.Copy).then_inc(wo_copied, 1)
            act.wait_ge(wc_ready, 1)
            act.activation(wc_t[:, :], bank[5][:, 0:P], ACT.Copy)
            act.activation(bias2[0:1, :], bank[5][0:1, P:2 * P], ACT.Copy).then_inc(wc_copied, 1)
            act.wait_ge(weights_loaded, 16 * 6)
            for c in range(NODE_COLS // GATE_COLS):
                act.wait_ge(prod_ready, c + 1)
                for n in range(GATE_COLS):
                    at = c * GATE_COLS + n
                    last = act.activation(gate_junk[0:NODE_ROWS], gate_prod[0:NODE_ROWS, n, :], ACT.Copy,
                                          accum_out=gate_sum[0:NODE_ROWS, at:at + 1])
                    act.drain()
                act.drain().then_inc(prod_used, 1)
            act.activation(node_rows[:, :, FEAT + 1], gate_sum[0:NODE_ROWS, :], ACT.Identity,
                           bias=bg[0:NODE_ROWS, 0:1]).then_inc(gates_ready, 1)
            for k, back, g, _ in turning:
                into = rows_a if back else turn_a
                for ps, at, n, filled in banks_of(k, back, g):
                    act.wait_ge(turned[g], filled)
                    act.activation(into[:, at:at + n], ps[:, 0:n], ACT.Copy).then_inc(turn_copied[g], 1)

            def copy_prep(i, par):
                act.wait_ge(prep_turned, i + 1)
                act.activation(gather_at[par][:, :], prep_ps[:, 0, :], ACT.Copy)
                act.activation(place_t[par][:, :], prep_ps[:, 1, :], ACT.Copy)
                act.activation(offs[par][:, :], tile_block_ps, ACT.Copy)
                act.activation(tile_pen[par][:, :], tile_pen_ps, ACT.Copy)
                act.drain().then_inc(prep_copied, 1)

            def weigh(i, par, tiles=slice(0, T)):
                act.wait_ge(expo_turned, i + 1)
                act.activation(weights[par][:, :, tiles], expo_ps[:, :, tiles], ACT.Exp).then_inc(weights_ready, 1)

            copy_prep(0, 0)
            act.wait_ge(bias_spread, 1)
            for c, n in ((0, 4), (4, GB - 4)):
                last = act.activation(bias_of[:, c:c + n, :], bank[c // 4][0:6 * GB, 0:n * P].rearrange("p (c f) -> p c f", f=P), ACT.Copy)
            last.then_inc(bias_copied, 1)
            with loop(ENGINE.Activation, 0, CHUNKS // 2 - 1) as j:
                for par in range(2):
                    copy_prep(2 * j + (par + 1), 1 - par)
                    weigh(2 * j + par, par)
            copy_prep(CHUNKS - 1, 1)
            weigh(CHUNKS - 2, 0)
            weigh(CHUNKS - 1, 1, slice(0, EARLY))
            weigh(CHUNKS, 1, slice(EARLY, T))

            def copy_pooled(g, par):
                act.wait_ge(pooled_turned, g + 1)
                for c, n in ((0, 4), (4, GB - 4)):
                    act.activation(pooled_t[par][:, c:c + n, :], bank[2 * par + c // 4][:, 0:n * P].rearrange("p (c f) -> p c f", f=P), ACT.Copy)
                act.activation(share_t[par][:, :], bank[2 * par + 1][0:6 * GB, 3 * P:], ACT.Copy)
                act.drain().then_inc(pooled_copied, 1)

            def take_root(g, par):
                act.wait_ge(var_ready, g + 1)
                act.activation(std[par][:, :], mean_var[par][:, :, 1], ACT.Sqrt, bias=eps_col[:, 0:1]).then_inc(std_ready, 1)

            def normalise(g, par, stores):
                act.wait_ge(norm_ready, g + 1)
                if stores is not None:
                    act.wait_ge(stored[par], stores)
                for c in range(GB):
                    last = act.activation(y_grp[par][:, c, :], resid[par][:, c, :], ACT.Identity,
                                          scale=inv_std[par][:, c:c + 1], bias=shift[par][:, c:c + 1])
                    if c in (3, GB - 1):
                        last.then_inc(normalised, 1)
                act.drain().then_inc(out_ready, 1)

            act.activation(std[0][:, 0:1], eps_col[:, :], ACT.Sqrt)
            copy_pooled(0, 0)
            copy_pooled(1, 1)

            def step(g, par, stores, more=True):
                take_root(g, par)
                if more:
                    copy_pooled(g + 2, par)
                normalise(g, par, stores)

            step(0, 0, None)
            step(1, 1, None)
            with loop(ENGINE.Activation, 1, GROUPS // 2 - 1) as j:
                step(2 * j, 0, 16 * j)
                step(2 * j + 1, 1, 16 * j)
            step(GROUPS - 2, 0, 16 * (GROUPS // 2 - 1), more=False)
            step(GROUPS - 1, 1, 16 * (GROUPS // 2 - 1), more=False)

        @block.tensor
        def _(pe):
            pe.wait_ge(weights_loaded, 16 * 6)
            pe.wait_ge(consts_ready, 1)
            pe.nop(nofuse=True)
            pe.transpose(bank[4][:, 0:P], wo_sb[:, :], ident[:, :]).then_inc(wo_turned, 1)
            pe.wait_ge(wo_copied, 1)
            pe.matmul(bank[5][:, 0:P], lhsT=wl_sb[:, :], rhs=wo_t[:, :], start=True, stop=True)
            pe.matmul(bank[5][0:1, P:2 * P], lhsT=bl_col[:, :], rhs=wo_t[:, :], start=True, stop=True).then_inc(wc_ready, 1)
            pe.wait_ge(onehots_ready, 1)

            for g in range(HGROUPS):
                last = pe.matmul(hist_ps, lhsT=onehot[:, g, 0:LO, :].rearrange("p c k -> p (c k)"),
                                 rhs=onehot[:, g, LO:LO + HI, :].rearrange("p c k -> p (c k)"),
                                 start=g == 0, stop=g == HGROUPS - 1)
            last.then_inc(hist_ready, 1)
            pe.wait_ge(spread_ready, 1)
            pe.matmul(count_ps, lhsT=ones[0:LO * HCOLS, :], rhs=hist_spread[:, :, :].rearrange("p h l -> p (h l)"),
                      start=True, stop=True).then_inc(counts_ready, 1)
            for k, back, g, steps in turning:
                if back:
                    from_ = (turn_a, turn_b)[min(k - LOG_COLS, LOG_ROWS) % 2]
                else:
                    from_ = (rows_a, rows_b)[max(0, k - LOG_BIG) % 2]
                pe.wait_ge(steps_done[g], steps)
                for ps, at, n, _ in banks_of(k, back, g):
                    for q in range(0, n, P):
                        last = pe.transpose(ps[:, q:q + P], from_[:, at + q:at + q + P], ident[:, :])
                    last.then_inc(turned[g], 1)
            pe.drain().then_inc(gather_buf_free, 2)

            def turn_prep(i):
                pe.wait_ge(prep_done, i + 1)
                if not (isinstance(i, int) and i == 0):
                    pe.wait_ge(prep_copied, i)
                pe.nop(nofuse=True)
                pe.transpose(prep_ps[:, 0, :], dst_f[:, :], ident[0:T, 0:T])
                pe.transpose(prep_ps[:, 1, :], place_f[:, :], ident[0:T, 0:T])
                pe.transpose(tile_block_ps, sums_at[:, :], ident[0:T, 0:T])

            def turn_pen(i, par):
                pe.transpose(tile_pen_ps, pen_tile[par][:, P - 1:P], ident[0:T, 0:T]).then_inc(prep_turned, 1)

            turn_prep(0)
            turn_pen(0, 0)
            pe.wait_ge(bias_split, 1)
            for c in range(GB):
                for k in range(3):
                    last = pe.matmul(bank[c // 4][0:6 * GB, (c % 4) * P:(c % 4 + 1) * P], lhsT=bias_at[:, c, k, :],
                                     rhs=bias_parts[:, k, :], start=k == 0, stop=k == 2)
            last.then_inc(bias_spread, 1)
            pe.wait_ge(bias_copied, 1)
            def turn_softmax(i, par, n=T):
                pe.nop(nofuse=True)
                pe.transpose(gate_rows[0:n], gathered_rows[par][:, 0:n, FEAT + 1], ident[:, :]).then_inc(gates_turned, 1)
                pe.wait_ge(run_max_done, i + 1)
                pe.nop(nofuse=True)
                pe.transpose(tile_max_ps[:, 0:n], run_max[0:n, P - 1:P], ident[0:n, 0:n]).then_inc(tile_max_turned, 1)
                pe.wait_ge(carry_done, i + 1)
                pe.nop(nofuse=True)
                pe.transpose(carry_ps[0:n], carry[0:1, 0:n], ident[0:1, 0:1]).then_inc(carry_turned, 1)
                pe.wait_ge(expo_done, i + 1)
                pe.nop(nofuse=True)
                pe.transpose(expo_ps[:, 0, 0:n], expo[0:n, 0, :], ident[0:n, 0:n])
                pe.transpose(expo_ps[:, 1, 0:n], expo[0:n, 1, :], ident[0:n, 0:n]).then_inc(expo_turned, 1)

            def sum_tiles(i, par, batches):
                for b in batches:
                    pe.wait_ge(spread_done, i * NB + (b + 1))
                    pe.wait_ge(sums_added, i * T + (b + 1) * BATCH)
                    for u in range(BATCH):
                        slot = (b % 2) * BATCH + u
                        last = pe.matmul(tile_ps(slot), lhsT=spread[:, slot, :],
                                         rhs=gathered_rows[par][:, b * BATCH + u, 0:WIDTH], start=True, stop=True)
                    last.then_inc(tiles_summed, 1)

            with loop(ENGINE.PE, 0, CHUNKS // 2 - 1) as j:
                for par in range(2):
                    i = 2 * j + par
                    turn_prep(i + 1)
                    turn_pen(i + 1, 1 - par)
                    pe.wait_ge(rows_gathered[par], 16 * T * j + 16 * T)
                    turn_softmax(i, par)
                    sum_tiles(i, par, range(NB))
                    pe.drain().then_inc(gather_buf_free, 1)
            turn_prep(CHUNKS - 1)
            turn_pen(CHUNKS - 1, 1)
            pe.wait_ge(rows_gathered[0], 16 * T * (CHUNKS // 2))
            turn_softmax(CHUNKS - 2, 0)
            sum_tiles(CHUNKS - 2, 0, range(NB))
            pe.wait_ge(rows_gathered[1], 16 * T * (CHUNKS // 2 - 1) + 16 * EARLY)
            turn_softmax(CHUNKS - 1, 1, EARLY)
            sum_tiles(CHUNKS - 1, 1, range(EARLY // BATCH))
            pe.wait_ge(late_gathered, 16 * (TILES - (CHUNKS - 1) * T - EARLY))
            turn_softmax(CHUNKS, 1)
            sum_tiles(CHUNKS - 1, 1, range(EARLY // BATCH, NB))

            def turn_pooled(g, par):
                pe.wait_ge(pooled_ready, g + 1)
                if g >= 2:
                    pe.wait_ge(pooled_copied, g - 1)
                for c in range(GB):
                    pe.transpose(bank[2 * par + c // 4][:, (c % 4) * P:(c % 4 + 1) * P], pooled[par][:, c, :], ident[:, :])
                if g == 0:
                    pe.wait_ge(share_ready, 1)
                pe.transpose(bank[2 * par + 1][0:6 * GB, 3 * P:], share[:, g * GB:(g + 1) * GB, :].rearrange("p c k -> p (c k)"),
                             ident[:, :]).then_inc(pooled_turned, 1)

            def project(g, par):
                pe.wait_ge(pooled_copied, g + 1)
                pe.wait_ge(y_used, g + 1)
                for c in range(GB):
                    to = bank[4 + 2 * par + c // 4][:, (c % 4) * P:(c % 4 + 1) * P]
                    pe.matmul(to, lhsT=pooled_t[par][:, c, :], rhs=wc_t[:, :], start=True, stop=False)
                    last = pe.matmul(to, lhsT=share_t[par][:, :], rhs=bias_of[:, c, :], start=False, stop=True)
                last.then_inc(y_ready, 1)

            turn_pooled(0, 0)
            turn_pooled(1, 1)
            for g in range(GROUPS):
                project(g, g % 2)
                if g + 2 < GROUPS:
                    turn_pooled(g + 2, g % 2)

        @block.vector
        def _(dve):
            dve.memset(zero_key[:, :], 0).then_inc(zero_ready, 1)
            dve.memset(turn_a[:, MAIN_COLS:EDGE_COLS], as_float(0x7FFF0000))
            dve.memset(turn_b[:, MAIN_COLS:EDGE_COLS], 0.0)
            dve.drain().then_inc(blank_ready, 1)
            dve.memset(rows_a[:, :], as_float(LAST_KEY))
            dve.memset(ones[:, :], 1.0)
            dve.memset(eps_col[:, :], 1e-5)
            dve.memset(carry[:, :], NEG)
            dve.wait_ge(iotas_ready, 1)
            dve.tensor_copy(iota_row[:, :], iota_i[:, :])
            dve.tensor_copy(part_idx[:, :], part_idx_i[:, :])
            dve.tensor_scalar(diag_eq[:, :, :], diag_i[:, :, :], 0.0, None, ALU.is_equal)
            dve.tensor_scalar(padkey_i[:, :], padkey_i[:, :], BLOCK_SHIFT, KEY_BASE | PAD_PLACE << DST_BITS,
                              ALU.logical_shift_left, ALU.bitwise_or)
            dve.memset(bit_i[:, 0:1], 1)
            dve.drain()
            dve.tensor_scalar(ident[:, :], iota_row[:, :], part_idx[:, 0:1], None, ALU.is_equal)
            dve.tensor_reduce(same_col[:, :], diag_eq[:, :, :], AX.X, ALU.add)
            dve.tensor_reduce(is_lo[:, :], diag_eq[:, :, :].rearrange("p k l -> p l k"), AX.X, ALU.add)
            for k in range(LOG_ROWS):
                dve.tensor_scalar(bit_i[:, k + 1:k + 2], part_idx_i[:, :], k, 1, ALU.logical_shift_right, ALU.bitwise_and)
            dve.drain()
            dve.tensor_scalar(signs[:, :], bit_i[:, :], 2.0, -1.0, ALU.mult, ALU.add)
            dve.drain().then_inc(consts_ready, 1)
            dve.tensor_tensor(flips[:, :], signs[:, 1:], signs[:, 0:LOG_ROWS], ALU.mult)

            e = slice(0, P), slice(0, EDGE_COLS)
            dve.wait_ge(src_loaded, 32)
            dve.tensor_scalar(part_i[e], src_i[e], P - 1, DST_BITS, ALU.bitwise_and, ALU.logical_shift_left)
            dve.tensor_scalar(part2_i, src_i[e], 7, BLOCK_SHIFT, ALU.logical_shift_right, ALU.logical_shift_left)
            dve.drain()
            dve.scalar_tensor_tensor(part_i[e], part_i[e], KEY_BASE, part2_i, ALU.bitwise_or, ALU.bitwise_or)
            dve.drain()
            dve.wait_ge(dst_loaded, 32)
            keys_i = rows_a.ap().bitcast(I32)
            for here in ((slice(0, P), slice(0, MAIN_COLS)), (slice(0, REST_ROWS), slice(MAIN_COLS, PAD_AT))):
                dve.tensor_tensor(keys_i[here], part_i[here], dst_i[here], ALU.bitwise_or)
            dve.drain()
            dve.tensor_scalar(part_i[e], src_i[e], 7, LO - 1, ALU.logical_shift_right, ALU.bitwise_and)
            dve.tensor_scalar(part2_i, src_i[e], 11, None, ALU.logical_shift_right)
            dve.drain()
            lo_b, hi_b = (lohi_b[:, k * EDGE_COLS:(k + 1) * EDGE_COLS].rearrange("p (g k) -> p g k", k=HCOLS) for k in range(2))
            dve.tensor_copy(lo_b, part_i[e].rearrange("p (g k) -> p g k", k=HCOLS))
            dve.tensor_copy(hi_b, part2_i.rearrange("p (g k) -> p g k", k=HCOLS))
            dve.drain()
            for c in range(LO):
                dve.tensor_scalar(onehot[:, :, c, :], lo_b, float(c), None, ALU.is_equal)
            for c in range(HI):
                dve.tensor_scalar(onehot[:, :, LO + c, :], hi_b, float(c), None, ALU.is_equal)
            dve.drain().then_inc(onehots_ready, 1)
            def prepare(i, j_uses, par):
                dve.wait_ge(k3_loaded[par], j_uses * 48 + 48)
                own = k3[par][:, 1, :]
                dve.tensor_scalar(node_i[:, :, :], k3[par][:, :, :], DST_BITS, None, ALU.logical_shift_right)
                dve.tensor_scalar(dst_r[:, :], own, DST_MASK, None, ALU.bitwise_and)
                dve.tensor_scalar(place_r[:, :], own, DST_BITS, PLACE_MASK, ALU.logical_shift_right, ALU.bitwise_and)
                dve.tensor_scalar(prev_place_i[:, :], k3[par][:, 0, 0:1], DST_BITS, PLACE_MASK, ALU.logical_shift_right, ALU.bitwise_and)
                dve.tensor_scalar(block_i[:, :], k3[par][:, 1, 0:1], BLOCK_SHIFT, 127, ALU.logical_shift_right, ALU.bitwise_and)
                dve.drain().then_inc(k3_used, 1)
                if not (isinstance(i, int) and i == 0):
                    dve.wait_ge(prep_turned, i)
                dve.tensor_copy(node_f[:, :, :], node_i[:, :, :])
                dve.tensor_copy(dst_f[:, :], dst_r[:, :])
                dve.tensor_copy(place_f[:, :], place_r[:, :])
                dve.tensor_copy(prev_place[par][:, :], prev_place_i[:, :])
                dve.tensor_scalar(sums_at[:, :], block_i[:, :], float(WIDTH), None, ALU.mult)
                dve.drain()
                dve.tensor_scalar(pen_tile[par][:, :], node_f[:, 1, :], node_f[:, 0, 0:1], NEG, ALU.not_equal, ALU.mult)
                dve.tensor_tensor(differs[:, :, :], node_f[:, 1:2, :].to_broadcast([T, 2, P]), node_f[:, 0:3:2, :], ALU.not_equal)
                dve.drain()
                dve.tensor_scalar(pen[par][:, :, :], differs[:, :, :], NEG, None, ALU.mult)
                dve.tensor_scalar(goes_on[par][:, :], pen_tile[par][:, 0:1], 0.0, None, ALU.is_equal)
                dve.drain().then_inc(prep_done, 1)

            rows, turns = (rows_a, rows_b), (turn_a, turn_b)
            done = [0, 0]

            def after_last(g):
                if done[g]:
                    dve.wait_ge(steps_done[g], done[g])

            def step_ends(g, ins):
                ins.then_inc(steps_done[g], 1)
                done[g] += 1

            def exchange_mirrored(g, a, b, k):
                va, vb = (v[:, cols_of(g)].rearrange("p (a t j) -> p a t j", t=2, j=1 << (k - 1)) for v in (a, b))
                after_last(g)
                dve.tensor_tensor(vb[:, :, 0, :], va[:, :, 0, :], va[:, :, 1, ::-1], ALU.min)
                step_ends(g, dve.tensor_tensor(vb[:, :, 1, :], va[:, :, 0, ::-1], va[:, :, 1, :], ALU.max))

            def exchange(g, a, b, s):
                va, vb = (v[:, cols_of(g)].rearrange("p (a t j) -> p a t j", t=2, j=1 << s) for v in (a, b))
                after_last(g)
                dve.tensor_tensor(vb[:, :, 0, :], va[:, :, 0, :], va[:, :, 1, :], ALU.min)
                step_ends(g, dve.tensor_tensor(vb[:, :, 1, :], va[:, :, 0, :], va[:, :, 1, :], ALU.max))

            def exchange_big(g, a, b, s):
                va, vb = (v[:, :].rearrange("p (b c) -> p b c", c=BCOLS) for v in (a, b))
                after_last(g)
                blocks = range(*PARTS[g])
                for n in blocks:
                    mate = n + (1 << s)
                    if not n >> s & 1 and mate < BIG:
                        dve.tensor_tensor(vb[:, n, :], va[:, n, :], va[:, mate, :], ALU.min)
                        ins = dve.tensor_tensor(vb[:, mate, :], va[:, n, :], va[:, mate, :], ALU.max)
                    elif not n >> s & 1:
                        ins = dve.tensor_copy(vb[:, n, :], va[:, n, :])
                step_ends(g, ins)

            def sign_of(k, n):
                return 1 if k == LOG_KEYS or n >> (k - LOG_BIG) & 1 else -1

            def set_signs(g, k):
                after_last(g)
                if k < LOG_BIG:
                    c = k - LOG_COLS
                    ins = dve.tensor_scalar(rows_a[:, cols_of(g)], rows_a[:, cols_of(g)], flips[:, c:c + 1], None, ALU.mult)
                elif k == LOG_BIG:
                    for n in range(*PARTS[g]):
                        here = rows_a[:, n * BCOLS:(n + 1) * BCOLS]
                        ins = dve.tensor_scalar(here, here, signs[:, LOG_ROWS:], float(sign_of(k, n)), ALU.mult, ALU.mult)
                else:
                    for n in range(*PARTS[g]):
                        if sign_of(k, n) != sign_of(k - 1, n):
                            here = rows_a[:, n * BCOLS:(n + 1) * BCOLS]
                            ins = dve.tensor_scalar(here, here, -1.0, None, ALU.mult)
                step_ends(g, ins)

            def short_phases(g):
                n = 0
                for k in range(1, LOG_COLS):
                    for s in reversed(range(k)):
                        if s == k - 1:
                            exchange_mirrored(g, rows[n % 2], rows[1 - n % 2], k)
                        else:
                            exchange(g, rows[n % 2], rows[1 - n % 2], s)
                        n += 1
                assert n % 2 == 0

            def sort_step(g, k, kind, n):
                if kind == "signs":
                    set_signs(g, k)
                elif kind == "big":
                    exchange_big(g, rows[n % 2], rows[1 - n % 2], k - LOG_BIG - 1 - n)
                elif kind == "turned":
                    if n == 0:
                        dve.wait_ge(turn_copied[g], 4 * (k - LOG_COLS - 1) + 2)
                    exchange(g, turns[n % 2], turns[1 - n % 2], min(k - LOG_COLS, LOG_ROWS) - 1 - n)
                else:
                    if n == 0 and k > LOG_COLS:
                        dve.wait_ge(turn_copied[g], 4 * (k - LOG_COLS - 1) + 4)
                    if k == LOG_COLS and n == 0:
                        exchange_mirrored(g, rows[0], rows[1], k)
                    else:
                        exchange(g, rows[n % 2], rows[1 - n % 2], LOG_COLS - 1 - n)

            def by_turns(steps, lag):
                for n in range(len(steps) + lag):
                    if n < len(steps):
                        sort_step(0, *steps[n])
                    if n >= lag:
                        sort_step(1, *steps[n - lag])

            short_phases(0)
            dve.wait_ge(hist_ready, 1)
            q = LO * HCOLS
            dve.tensor_tensor(hist_kept[:, :, :], hist_ps, same_col[:, :].unsqueeze(1).to_broadcast([q, HI, HCOLS]), ALU.mult)
            dve.drain()
            dve.tensor_reduce(hist_sum[:, :], hist_kept[:, :, :], AX.X, ALU.add)
            dve.drain()
            dve.tensor_tensor(hist_spread[:, :, :], hist_sum[:, :].unsqueeze(2).to_broadcast([q, HI, LO]),
                              is_lo[:, :].unsqueeze(1).to_broadcast([q, HI, LO]), ALU.mult).then_inc(spread_ready, 1)
            dve.wait_ge(counts_ready, 1)
            dve.tensor_scalar(padn_i[:, :], count_ps[:, 0:BLOCKS], -1.0, None, ALU.mult)
            dve.drain()
            dve.tensor_scalar(padn_j[:, :], padn_i[:, :], P - 1, None, ALU.bitwise_and)
            dve.drain()
            dve.tensor_scalar(pad_off[:, :], padn_j[:, :], part_idx[:, 0:1], as_float(LAST_KEY), ALU.is_le, ALU.mult)
            dve.drain()
            dve.tensor_tensor(rows_a[:, PAD_AT:PAD_AT + BLOCKS], padkey_i.ap().bitcast(F32), pad_off[:, :], ALU.max)
            dve.drain()

            short_phases(1)

            def kinds(k, lengths):
                return [(k, kind, n) for kind, length in lengths for n in range(length)]

            def in_rows(k):
                return kinds(k, (("rows", LOG_COLS),)) + kinds(k + 1, (("signs", 1), ("big", max(0, k + 1 - LOG_BIG))))

            by_turns(kinds(LOG_COLS, (("signs", 1),)), LAG)
            for k in range(LOG_COLS, LOG_KEYS - 1):
                by_turns(in_rows(k), LAG)
                by_turns(kinds(k + 1, (("turned", min(k + 1 - LOG_COLS, LOG_ROWS)),)), LAG)
            by_turns(kinds(LOG_KEYS - 1, (("rows", LOG_COLS),)), LAG)
            set_signs(0, LOG_KEYS)
            for g in range(2):
                after_last(g)
            for n in range(BIG - 4):
                a0, a1, b0, b1 = (v[:, m * BCOLS:(m + 1) * BCOLS] for v in (rows_a, rows_b) for m in (n, n + 4))
                dve.tensor_tensor(b0, a0, a1, ALU.min)
                dve.tensor_tensor(b1, a0, a1, ALU.max)
            alone = slice((BIG - 4) * BCOLS, 4 * BCOLS)
            step_ends(0, dve.tensor_copy(rows_b[:, alone], rows_a[:, alone]))
            dve.drain().then_inc(steps_done[1], 2)
            done[1] += 2
            big = kinds(LOG_KEYS, (("big", LOG_KEYS - LOG_BIG),))[1:]
            by_turns(big, LAG)
            last_turned, last_rows = kinds(LOG_KEYS, (("turned", LOG_ROWS),)), kinds(LOG_KEYS, (("rows", LOG_COLS),))
            for g, steps in ((0, last_turned), (1, last_turned[:LAG + 1]), (0, last_rows), (1, last_turned[LAG + 1:] + last_rows[:1])):
                for step in steps:
                    sort_step(g, *step)
            prepare(0, 0, 0)
            for step in last_rows[1:]:
                sort_step(1, *step)
            assert done == [all_steps, all_steps]
            dve.wait_ge(sums_blank, 1)
            dve.drain().then_inc(sums_added, 2 * BATCH)

            def softmax(i, par, n=T):
                dve.wait_ge(gates_turned, i + 1)
                dve.tensor_tensor_scan(run_max[0:n, :], pen[par][0:n, 0, :], gate_rows[0:n], NEG, ALU.add, ALU.max)
                dve.drain().then_inc(run_max_done, 1)
                dve.wait_ge(tile_max_turned, i + 1)
                dve.tensor_tensor_scan(carry[0:1, 1:n + 1], tile_pen[par][:, 0:n], tile_max_ps[:, 0:n], carry[0:1, 0:1], ALU.add, ALU.max)
                dve.drain().then_inc(carry_done, 1)
                dve.wait_ge(carry_turned, i + 1)
                dve.tensor_copy(carry_col[0:n, :], carry_ps[0:n])
                if n == T:
                    dve.tensor_copy(carry[0:1, 0:1], carry[0:1, T:T + 1])
                dve.drain()
                dve.scalar_tensor_tensor(run_max2[0:n, :], pen_tile[par][0:n, :], carry_col[0:n, 0:1], run_max[0:n, :], ALU.add, ALU.max)
                dve.drain()
                dve.tensor_tensor_scan(seg_max[0:n, ::-1], pen[par][0:n, 1, ::-1], run_max2[0:n, ::-1], NEG, ALU.add, ALU.max)
                dve.drain()
                dve.tensor_tensor(expo[0:n, 0, :], gate_rows[0:n], seg_max[0:n, :], ALU.subtract)
                dve.scalar_tensor_tensor(drop[0:n, :], carry_col[0:n, :], seg_max[0:n, 0:1], goes_on[par][0:n, :], ALU.subtract, ALU.mult)
                dve.drain()
                dve.tensor_scalar(expo[0:n, 1, :], iota_row[0:n, :], prev_place[par][0:n, 0:1], drop[0:n, 0:1], ALU.is_equal, ALU.mult)
                dve.drain().then_inc(expo_done, 1)

            def spread_tile(par, t, slot):
                return dve.tensor_scalar(spread[:, slot, :], iota_row[:, :], place_t[par][:, t:t + 1],
                                         weights[par][:, 0, t:t + 1], ALU.is_equal, ALU.mult)

            def add_tile(i, par, t, slot, at_col):
                here = sums[:, bass.ds(at_col, WIDTH)]
                dve.wait_ge(sums_added, i * T + (t + 2 * BATCH))
                dve.scalar_tensor_tensor(here, here, weights[par][:, 1, t:t + 1], tile_ps(slot), ALU.mult, ALU.add).then_inc(sums_added, 1)

            dve.wait_ge(bias_iota_ready, 1)
            dve.tensor_scalar(bias_at[:, :, :, :], bias_at_i[:, :, :, :], 0.0, None, ALU.is_equal)
            dve.wait_ge(wc_copied, 1)
            left = bias2[:, :]
            for k in range(3):
                dve.tensor_copy(bias_part_b[:, :], left)
                dve.drain()
                dve.tensor_copy(bias_parts[:, k, :], bias_part_b[:, :])
                dve.drain()
                if k < 2:
                    dve.tensor_tensor(bias_left[:, k, :], left, bias_parts[:, k, :], ALU.subtract)
                    left = bias_left[:, k, :]
                    dve.drain()
            dve.drain().then_inc(bias_split, 1)
            dve.memset(share[:, :, 3:6], 1.0)

            def add_tiles(i, softmaxes, par, batches):
                dve.wait_ge(weights_ready, softmaxes)
                dve.wait_ge(prep_copied, i + 1)
                dve.nop(nofuse=True)
                at_cols = {}
                first, end = batches[0], batches[-1] + 1
                for b in range(first, end + 2):
                    if b < end and (b - first) % 2 == 0:
                        n = min(2, end - b) * BATCH
                        got = nc.values_load_multi_w_load_instructions(
                            offs[par][0:1, b * BATCH:b * BATCH + n], engines=[mybir.EngineType.DVE], min_val=0,
                            max_val=(BLOCKS - 1) * WIDTH, skip_runtime_bounds_check_because="a block times the width")[1]
                        at_cols.update({b * BATCH + k: got[k] for k in range(n)})
                    if b >= first + 2:
                        dve.wait_ge(tiles_summed, i * NB + (b - 1))
                    for u in range(BATCH):
                        slot = (b % 2) * BATCH + u
                        if b < end:
                            ins = spread_tile(par, b * BATCH + u, slot)
                            if u == BATCH - 1:
                                ins.then_inc(spread_done, 1)
                        if b >= first + 2:
                            t = (b - 2) * BATCH + u
                            add_tile(i, par, t, slot, at_cols[t])

            with loop(ENGINE.DVE, 0, CHUNKS // 2 - 1) as j:
                for par in range(2):
                    i = 2 * j + par
                    prepare(i + 1, j + par, 1 - par)
                    softmax(i, par)
                    add_tiles(i, i + 1, par, range(NB))
            prepare(CHUNKS - 1, CHUNKS // 2 - 1, 1)
            softmax(CHUNKS - 2, 0)
            add_tiles(CHUNKS - 2, CHUNKS - 1, 0, range(NB))
            softmax(CHUNKS - 1, 1, EARLY)
            add_tiles(CHUNKS - 1, CHUNKS, 1, range(EARLY // BATCH))
            softmax(CHUNKS, 1)
            add_tiles(CHUNKS - 1, CHUNKS + 1, 1, range(EARLY // BATCH, NB))

            dve.drain()
            dens = sums.rearrange("p (b w) -> p b w", w=WIDTH)[:, :, FEAT]
            dve.tensor_scalar(inv_den, dens, 1e-16, None, ALU.add)
            dve.drain()
            dve.reciprocal(inv_den, inv_den)
            dve.drain().then_inc(dens_ready, 1)
            dve.tensor_tensor(ratio, dens, inv_den, ALU.mult)
            dve.drain()
            dve.tensor_scalar(share[:, :, 0:3], ratio.unsqueeze(2).to_broadcast([P, BLOCKS, 3]), 0.5, None, ALU.is_gt)
            dve.drain().then_inc(share_ready, 1)
            dve.drain().then_inc(y_used, 2)

            def add_x(g, par, x_count, peeled=None):
                dve.wait_ge(x_in[par], x_count)
                dve.wait_ge(y_ready, g + 1)
                for c, n in ((0, 4), (4, GB - 4)):
                    if peeled != "first":
                        dve.wait_ge(normalised, 2 * g - 3 + c // 4)
                    ps = bank[4 + 2 * par + c // 4][:, 0:n * P].rearrange("p (c f) -> p c f", f=P)
                    dve.tensor_tensor(resid[par][:, c:c + n, :], ps, x_grp[par][:, c:c + n, :], ALU.add)
                dve.drain().then_inc(y_used, 1)

            def measure(g, par):
                for c in range(GB):
                    dve.bn_stats(stats[:, c, :], resid[par][:, c, :])
                dve.drain()
                for c in range(GB):
                    dve.bn_aggr(mean_var[par][:, c, :], stats[:, c, :])
                dve.drain().then_inc(var_ready, 1)

            def scale_and_shift(g, par):
                dve.wait_ge(std_ready, g + 1)
                dve.reciprocal(inv_std[par][:, :], std[par][:, :])
                dve.drain()
                dve.scalar_tensor_tensor(shift[par][:, :], mean_var[par][:, :, 0], -1.0, inv_std[par][:, :], ALU.mult, ALU.mult)
                dve.drain().then_inc(norm_ready, 1)

            def step(g, par, x_count, peeled=None):
                add_x(g, par, x_count, peeled)
                if not (isinstance(g, int) and g == 0):
                    scale_and_shift(g - 1, 1 - par)
                measure(g, par)

            step(0, 0, 16, "first")
            step(1, 1, 16, "first")
            with loop(ENGINE.DVE, 1, GROUPS // 2 - 1) as j:
                step(2 * j, 0, 16 * j + 16)
                step(2 * j + 1, 1, 16 * j + 16)
            step(GROUPS - 2, 0, 16 * (GROUPS // 2))
            step(GROUPS - 1, 1, 16 * (GROUPS // 2 + 1))
            scale_and_shift(GROUPS - 1, 1)


_INS = ['x', 'src', 'dst', 'L0_gnn_W_lin', 'L0_gnn_b_lin', 'L0_gnn_W_gate', 'L0_gnn_b_gate', 'L0_gnn_W_out', 'L0_gnn_b_out']


def kernel(**inputs):
    import concourse.bacc as bacc
    from concourse.bass_utils import run_bass_kernel_spmd as run
    nc = bacc.Bacc("TRN2", target_bir_lowering=False, num_devices=1)
    arrays, args = {}, []
    for name in _INS:
        a = np.ascontiguousarray(inputs[name])
        arrays[f"in_{name}"] = a
        args.append(nc.dram_tensor(f"in_{name}", a.shape, mybir.dt.from_np(a.dtype), kind="ExternalInput").ap())
    out = nc.dram_tensor("out_0", (NODES, FEAT), F32, kind="ExternalOutput").ap()
    graph_attention(nc, *args, out)
    r = run(nc, [arrays], core_ids=[0])
    return r.results[0]["out_0"]
```
